# Optimizing a Trainium2 kernel written in Bass

```python
import numpy as np
import jax
import jax.numpy as jnp

def _softmax(x, axis=-1):
    return jax.nn.softmax(x, axis=axis)

def _gelu(x):
    return jax.nn.gelu(x, approximate=True)

def _silu(x):
    return jax.nn.silu(x)

def _sigmoid(x):
    return jax.nn.sigmoid(x)

def _layernorm(x, axis=-1, eps=1e-05):
    m = jnp.mean(x, axis=axis, keepdims=True)
    v = jnp.var(x, axis=axis, keepdims=True)
    return (x - m) / jnp.sqrt(v + eps)

def _scatter_add(tgt, idx, src, axis=0):
    return tgt.at[idx].add(src)

def _segment_sum(src, seg, n):
    return jax.ops.segment_sum(src, seg, n)
kernel_name = 'mk_adj_resnorm_d2_adj_r2_6dec98'

def setup_inputs(seed: int=0):
    np.random.seed(seed)
    _w = jnp.asarray

    def _rec_inputs():
        import jax
        import jax.numpy as jnp
        _gk = jax.random.key(seed)
        x = -0.0004039 + 1 * jax.random.normal(jax.random.fold_in(_gk, 1), (32, 256, 384), jnp.float32)
        _w = (1.0 + jnp.arange(256, dtype=jnp.float32)) ** (-0.5)
        _w = _w / _w.mean()
        _pij = jnp.clip(0.03125 * _w[:, None] * _w[None, :], 0.0, 1.0)
        _a = jax.random.uniform(jax.random.fold_in(_gk, 2), (32, 256, 256)) < _pij
        _af = _a.astype(jnp.float32)
        adj = _af
        return (x, adj)
    x, adj = _rec_inputs()

    def _L0_gnn_setup():
        import jax, jax.numpy as jnp
        import numpy as np
        B, S, H, L = (32, 256, 384, 2)

        def _layer_norm(z, a, b, eps=0.001):
            mu = jnp.mean(z, axis=-1, keepdims=True)
            sigma = jnp.std(z, axis=-1, keepdims=True, ddof=1)
            return (z - mu) / (sigma + eps) * a + b
        key = jax.random.key(seed)
        ks = jax.random.split(key, 6)
        hidden_state = jax.random.normal(ks[0], (B, S, H), dtype=jnp.float32)
        adjacency_matrix = (jax.random.uniform(ks[1], (B, S, S)) < 0.2).astype(jnp.float32)
        W_left = 0.05 * jax.random.normal(ks[2], (L, H, H), dtype=jnp.float32)
        W_right = 0.05 * jax.random.normal(ks[3], (L, H, H), dtype=jnp.float32)
        W_lin = 0.05 * jax.random.normal(ks[4], (L, H, H), dtype=jnp.float32)
        b_lin = jnp.zeros((L, H), dtype=jnp.float32)
        ln_a = jnp.ones((L, H), dtype=jnp.float32)
        ln_b = jnp.zeros((L, H), dtype=jnp.float32)
        return {'hidden_state': hidden_state, 'adjacency_matrix': adjacency_matrix, 'W_left': W_left, 'W_right': W_right, 'W_lin': W_lin, 'b_lin': b_lin, 'ln_a': ln_a, 'ln_b': ln_b}
    _L0_gnn_all = _L0_gnn_setup()
    _L0_gnn_in = {k: v for k, v in _L0_gnn_all.items() if k in ('W_left', 'W_right', 'W_lin', 'b_lin', 'ln_a', 'ln_b')}
    del _L0_gnn_all

    def _L1_gnn_setup():
        import jax, jax.numpy as jnp
        import numpy as np
        LN_EPS = 1e-12

        def _digcn_forward(hidden_state, adjacency_matrix, Wl, bl, Ws, bs, Wr, br, ln_w, ln_b):
            B, S, D = hidden_state.shape
            temper = jnp.asarray(D, jnp.float32) ** 0.5
            i = jnp.arange(S)
            upper = (i[None, :] > i[:, None]).astype(hidden_state.dtype)
            lower = (i[None, :] < i[:, None]).astype(hidden_state.dtype)

            def layer(h, params):
                wl, b_l, ws, b_s, wr, b_r, g, beta = params
                u = jnp.einsum('bid,bjd->bij', h, h) / temper
                a = jax.nn.softmax(u, axis=-1)
                delta = a * adjacency_matrix
                attn = delta / (jnp.sum(delta, axis=-1, keepdims=True) + 1e-10)
                hl = h @ wl.T + b_l
                hs = h @ ws.T + b_s
                hr = h @ wr.T + b_r
                diag_a = jnp.diagonal(attn, axis1=1, axis2=2)
                ctx = jnp.einsum('bij,bjd->bid', attn * upper, hl) + diag_a[..., None] * hs + jnp.einsum('bij,bjd->bid', attn * lower, hr)
                mean = ctx.mean(-1, keepdims=True)
                var = ctx.var(-1, keepdims=True)
                o = (ctx - mean) / jnp.sqrt(var + LN_EPS) * g + beta
                return (jax.nn.relu(o), None)
            out, _ = jax.lax.scan(layer, hidden_state, (Wl, bl, Ws, bs, Wr, br, ln_w, ln_b))
            return out
        key = jax.random.key(seed)
        ks = jax.random.split(key, 6)
        B, S, D, L = (8, 512, 384, 2)
        scale = (1.0 / D) ** 0.5
        hidden_state = jax.random.normal(ks[0], (B, S, D), jnp.float32)
        adjacency_matrix = (jax.random.uniform(ks[1], (B, S, S)) < 0.05).astype(jnp.float32)
        Wl = jax.random.normal(ks[2], (L, D, D), jnp.float32) * scale
        Ws = jax.random.normal(ks[3], (L, D, D), jnp.float32) * scale
        Wr = jax.random.normal(ks[4], (L, D, D), jnp.float32) * scale
        bl = jnp.zeros((L, D), jnp.float32)
        bs = jnp.zeros((L, D), jnp.float32)
        br = jnp.zeros((L, D), jnp.float32)
        ln_w = jnp.ones((L, D), jnp.float32)
        ln_b = jnp.zeros((L, D), jnp.float32)
        return dict(hidden_state=hidden_state, adjacency_matrix=adjacency_matrix, Wl=Wl, bl=bl, Ws=Ws, bs=bs, Wr=Wr, br=br, ln_w=ln_w, ln_b=ln_b)
    _L1_gnn_all = _L1_gnn_setup()
    _L1_gnn_in = {k: v for k, v in _L1_gnn_all.items() if k in ('Wl', 'bl', 'Ws', 'bs', 'Wr', 'br', 'ln_w', 'ln_b')}
    del _L1_gnn_all
    return {'x': x, 'adj': adj, 'L0_gnn_W_left': _L0_gnn_in['W_left'], 'L0_gnn_W_right': _L0_gnn_in['W_right'], 'L0_gnn_W_lin': _L0_gnn_in['W_lin'], 'L0_gnn_b_lin': _L0_gnn_in['b_lin'], 'L0_gnn_ln_a': _L0_gnn_in['ln_a'], 'L0_gnn_ln_b': _L0_gnn_in['ln_b'], 'L1_gnn_Wl': _L1_gnn_in['Wl'], 'L1_gnn_bl': _L1_gnn_in['bl'], 'L1_gnn_Ws': _L1_gnn_in['Ws'], 'L1_gnn_bs': _L1_gnn_in['bs'], 'L1_gnn_Wr': _L1_gnn_in['Wr'], 'L1_gnn_br': _L1_gnn_in['br'], 'L1_gnn_ln_w': _L1_gnn_in['ln_w'], 'L1_gnn_ln_b': _L1_gnn_in['ln_b']}

def reference(x, adj, L0_gnn_W_left, L0_gnn_W_right, L0_gnn_W_lin, L0_gnn_b_lin, L0_gnn_ln_a, L0_gnn_ln_b, L1_gnn_Wl, L1_gnn_bl, L1_gnn_Ws, L1_gnn_bs, L1_gnn_Wr, L1_gnn_br, L1_gnn_ln_w, L1_gnn_ln_b):
    import jax
    import jax.numpy as jnp

    def _L0_gnn_ref(hidden_state, adjacency_matrix, W_left, W_right, W_lin, b_lin, ln_a, ln_b):
        import jax, jax.numpy as jnp
        import numpy as np
        B, S, H, L = (32, 256, 384, 2)

        def _layer_norm(z, a, b, eps=0.001):
            mu = jnp.mean(z, axis=-1, keepdims=True)
            sigma = jnp.std(z, axis=-1, keepdims=True, ddof=1)
            return (z - mu) / (sigma + eps) * a + b
        temper = float(np.sqrt(H))
        adj = adjacency_matrix
        adj_tri = jnp.triu(adj, k=1)
        diag_mask = jnp.triu(adj, k=0) - adj_tri
        h = hidden_state
        for l in range(L):
            m_left = jnp.einsum('bsh,oh->bso', h, W_left[l])
            m_right = jnp.einsum('bsh,oh->bso', h, W_right[l])
            u_left = jnp.einsum('bih,bjh->bij', h, m_left) / temper
            u_right = jnp.einsum('bih,bjh->bij', h, m_right) / temper
            u = u_left * adj_tri + u_left * diag_mask + u_right * jnp.swapaxes(adj_tri, 1, 2)
            delta_exp_u = jnp.exp(u) * adj
            attention = delta_exp_u / (jnp.sum(delta_exp_u, axis=2, keepdims=True) + 1e-10)
            h_lin = jnp.einsum('bsh,oh->bso', h, W_lin[l]) + b_lin[l]
            ctx = jnp.matmul(attention, h_lin)
            h = jax.nn.relu(_layer_norm(ctx, ln_a[l], ln_b[l]))
        return h

    def _L1_gnn_ref(hidden_state, adjacency_matrix, Wl, bl, Ws, bs, Wr, br, ln_w, ln_b):
        import jax, jax.numpy as jnp
        import numpy as np
        LN_EPS = 1e-12

        def _digcn_forward(hidden_state, adjacency_matrix, Wl, bl, Ws, bs, Wr, br, ln_w, ln_b):
            B, S, D = hidden_state.shape
            temper = jnp.asarray(D, jnp.float32) ** 0.5
            i = jnp.arange(S)
            upper = (i[None, :] > i[:, None]).astype(hidden_state.dtype)
            lower = (i[None, :] < i[:, None]).astype(hidden_state.dtype)

            def layer(h, params):
                wl, b_l, ws, b_s, wr, b_r, g, beta = params
                u = jnp.einsum('bid,bjd->bij', h, h) / temper
                a = jax.nn.softmax(u, axis=-1)
                delta = a * adjacency_matrix
                attn = delta / (jnp.sum(delta, axis=-1, keepdims=True) + 1e-10)
                hl = h @ wl.T + b_l
                hs = h @ ws.T + b_s
                hr = h @ wr.T + b_r
                diag_a = jnp.diagonal(attn, axis1=1, axis2=2)
                ctx = jnp.einsum('bij,bjd->bid', attn * upper, hl) + diag_a[..., None] * hs + jnp.einsum('bij,bjd->bid', attn * lower, hr)
                mean = ctx.mean(-1, keepdims=True)
                var = ctx.var(-1, keepdims=True)
                o = (ctx - mean) / jnp.sqrt(var + LN_EPS) * g + beta
                return (jax.nn.relu(o), None)
            out, _ = jax.lax.scan(layer, hidden_state, (Wl, bl, Ws, bs, Wr, br, ln_w, ln_b))
            return out
        return _digcn_forward(hidden_state, adjacency_matrix, Wl, bl, Ws, bs, Wr, br, ln_w, ln_b)
    x = _layernorm(x + _L0_gnn_ref(x, adj, L0_gnn_W_left, L0_gnn_W_right, L0_gnn_W_lin, L0_gnn_b_lin, L0_gnn_ln_a, L0_gnn_ln_b), axis=-1)
    x = _layernorm(x + _L1_gnn_ref(x, adj, L1_gnn_Wl, L1_gnn_bl, L1_gnn_Ws, L1_gnn_bs, L1_gnn_Wr, L1_gnn_br, L1_gnn_ln_w, L1_gnn_ln_b), axis=-1)
    return x

_drawn_inputs = setup_inputs


def setup_inputs(seed=0):
    import zlib

    import numpy as np

    out = dict(_drawn_inputs(seed))
    spreads = {'L0_gnn_b_lin': (0.0, 0.1),
     'L0_gnn_ln_a': (1.0, 0.2),
     'L0_gnn_ln_b': (0.0, 0.1),
     'L1_gnn_bl': (0.0, 0.1),
     'L1_gnn_bs': (0.0, 0.365),
     'L1_gnn_br': (0.0, 0.1),
     'L1_gnn_ln_w': (1.0, 0.2),
     'L1_gnn_ln_b': (0.0, 0.1)}
    factors = {}
    for name, (base, spread) in spreads.items():
        noise = np.random.default_rng([zlib.crc32(name.encode()), seed]).standard_normal(out[name].shape)
        drawn = base * np.exp(spread * noise) if base else spread * noise
        out[name] = jnp.asarray(drawn.astype(out[name].dtype))
    for name, factor in factors.items():
        out[name] = (out[name] * factor).astype(out[name].dtype)
    return out
```

```python
import concourse.bass as bass
from concourse import mybir
from contextlib import ExitStack

F32 = mybir.dt.float32
F32R = mybir.dt.float32r
I8 = mybir.dt.int8
ALU = mybir.AluOpType
ACT = mybir.ActivationFunctionType
AX = mybir.AxisListType

P = 128
B, S, D = 32, 256, 384
ROWS = S // P
KC = D // P
STREAMS = 2
PAIRS = B // STREAMS
LAYERS = 4
VW = D + 2
SCALE = 1.0 / float(D) ** 0.5
GEMM_BANKS = 4
BANK = 512

SCORE, PROJECT, VALUE, CONTEXT, TURN = "score", "project", "value", "context", "turn"
LEFT, SELF, RIGHT, TURN_PROBS = "value_left", "value_self", "value_right", "turn_probs"
GROUPS = {PROJECT: 3, VALUE: 2, LEFT: 2, SELF: 2, RIGHT: 2}


def groups(stage, layer):
    if stage == SCORE:
        return 2 if layer < 2 else 1
    return GROUPS.get(stage, 0)


def order():
    first = lambda l: [PROJECT] if l < 2 else [SCORE, LEFT]
    second = lambda l: [VALUE] if l < 2 else [SELF]
    third = lambda l: [SCORE] if l < 2 else [RIGHT, TURN_PROBS]
    out = []
    for l in range(LAYERS):
        out += [(k, l, 0) for k in first(l)]
        out += [(CONTEXT, l - 1, 1)] if l else []
        out += [(k, l, 0) for k in second(l)]
        out += [(TURN, l - 1, 1)] if l else []
        out += [(k, l, 0) for k in third(l)]
        out += [(k, l, 1) for k in first(l)]
        out += [(CONTEXT, l, 0)]
        out += [(k, l, 1) for k in second(l)]
        out += [(TURN, l, 0)] if l < LAYERS - 1 else []
        out += [(k, l, 1) for k in third(l)]
    return out + [(TURN, LAYERS - 1, 0), (TURN, LAYERS - 1, 1), (CONTEXT, LAYERS - 1, 1)]


ORDER = order()


def ordinals(kinds, weight=lambda stage, layer: 1):
    at, n = {}, 0
    for item in ORDER:
        if item[0] in kinds:
            at[item] = n
            n += weight(item[0], item[1])
    return at, n


GEMM_AT, GEMM_N = ordinals((PROJECT, VALUE, SCORE, LEFT, SELF, RIGHT), groups)
HI_AT, HI_N = ordinals((PROJECT, VALUE, LEFT, RIGHT), groups)
TURN_AT, TURN_N = ordinals((TURN, TURN_PROBS))
POW_AT, POW_N = ordinals((CONTEXT,), lambda stage, layer: 1 + layer % 2)
STEPS = {(SCORE, 0): 2, (SCORE, 1): 1, (SCORE, 2): 3, (SCORE, 3): 1, (LEFT, 2): 3, (LEFT, 3): 3,
         (TURN, 0): 1, (TURN, 2): 1, (CONTEXT, 0): 6, (CONTEXT, 1): 13, (CONTEXT, 2): 6, (CONTEXT, 3): 16}
DVE_STEPS = sum(STEPS.get(item[:2], 0) for item in ORDER)
assert GEMM_N % GEMM_BANKS == 0
BANK_N = GEMM_N // GEMM_BANKS


def build(nc, x_d, adj_d, adjT_d, w_d, bias_d, lncol_d, lnrow_d, out_d):
    ctx = ExitStack()
    with ctx:
        def sb(name, shape, dt=F32):
            return ctx.enter_context(nc.sbuf_tensor(name, shape, dt))

        def ps(name, shape):
            return ctx.enter_context(nc.psum_tensor(name, shape, F32))

        def sem(name):
            return ctx.enter_context(nc.semaphore(name))

        NW = 12
        w_hi = sb("w_hi", [P, NW, KC, D], F32R)
        w_lo = sb("w_lo", [P, NW, KC, D], F32R)
        NBIAS = 8
        bias_f = sb("bias_f", [2 * NBIAS, D])
        bias_pair = sb("bias_pair", [2 * NBIAS, D], F32R)
        bias_neg = bias_pair_tmp = sb("bias_neg", [2 * NBIAS, D], F32R)
        pick = sb("pick", [2 * NBIAS, NBIAS, P], F32R)
        pick_f = sb("pick_f", [2 * NBIAS, NBIAS])
        half_sel = sb("half_sel", [2 * NBIAS, 1])
        ln_rows = sb("ln_rows", [P, 2, 2, D])
        ln_cols = sb("ln_cols", [P, 2, 2, KC])
        ident = sb("ident", [P, P])
        from_adj = sb("from_adj", [P, ROWS, S], I8)
        take_side = sb("take_side", [P, ROWS, P], I8)
        exps = sb("exps", [P, 2, 2])

        proj = sb("proj", [P, 2, 6 * S + 8], F32R)
        scores = sb("scores", [P, ROWS, S])
        probsT = sb("probsT", [P, 2, 6 * P], F32R)

        per = range(STREAMS)
        arena = sb("arena", [P, 2 * STREAMS, ROWS * D])
        z = [arena[:, s, :].rearrange("p (r d) -> p r d", r=ROWS) for s in per]
        work = [arena[:, STREAMS + s, :] for s in per]
        hT = [sb(f"hT{s}", [P, 2, KC, S], F32R) for s in per]
        val = [sb(f"val{s}", [P, 2, ROWS, VW], F32R) for s in per]
        adj = [sb(f"adj{s}", [P, ROWS, S]) for s in per]
        adjT = [sb(f"adjT{s}", [P, ROWS, S]) for s in per]
        sym = [sb(f"sym{s}", [P, ROWS, S]) for s in per]
        x_in = [sb(f"x_in{s}", [P, ROWS, D]) for s in per]
        x_mid = [sb(f"x_mid{s}", [P, ROWS, D]) for s in per]
        small = [sb(f"small{s}", [P, 64]) for s in per]
        junk = sb("junk", [P, ROWS, P])

        val_r = proj[:, :, 0:ROWS * VW].rearrange("p h (r v) -> p h r v", r=ROWS)

        def col(s, first, n=ROWS):
            return small[s][:, first:first + n]
        STATS, MV, ROOT, RS, NB, EPS, DEN = 0, 12, 16, 18, 20, 22, 24
        ADIAG, PDIAG, Z, NMAX, MAXV, QSUM, VARP = 26, 28, 30, 32, 34, 36, 38

        def stats(s, r):
            return small[s][:, STATS + 6 * r:STATS + 6 * r + 6]

        def mean(s, r):
            return small[s][:, MV + 2 * r:MV + 2 * r + 1]

        def means(s):
            return small[s][:, MV:MV + 4].rearrange("p (r c) -> p r c", c=2)[:, :, 0]

        def variances(s):
            return small[s][:, MV:MV + 4].rearrange("p (r c) -> p r c", c=2)[:, :, 1]

        gemm_ps = [ps(f"gemm_ps{b}", [P, BANK]) for b in range(GEMM_BANKS)]
        turn_ps = ps("turn_ps", [P, 2 * BANK])
        ctx_ps = ps("ctx_ps", [P, ROWS, BANK])
        row_sums = ctx_ps[:, :, D]

        x_loaded = [sem(f"x_loaded{s}") for s in per]
        adj_loaded = [sem(f"adj_loaded{s}") for s in per]
        resid_used = [sem(f"resid_used{s}") for s in per]
        adj_used = [sem(f"adj_used{s}") for s in per]
        adjT_used = [sem(f"adjT_used{s}") for s in per]
        tri_ready = [sem(f"tri_ready{s}") for s in per]
        w_loaded = [sem(f"w_loaded{i}") for i in range(2)]
        w_hi_done = sem("w_hi_done")
        w_ready = sem("w_ready")
        const_loaded = sem("const_loaded")
        pool_const = sem("pool_const")
        pool_step = sem("pool_step")
        waited = sem("waited")
        bias_ready = sem("bias_ready")
        gemm_filled = sem("gemm_filled")
        gemm_free = [sem(f"gemm_free{b}") for b in range(GEMM_BANKS)]
        hi_done = sem("hi_done")
        max_ready = sem("max_ready")
        exp_done = sem("exp_done")
        probs_ready = sem("probs_ready")
        probsT_ready = sem("probsT_ready")
        turn_filled = sem("turn_filled")
        turn_hi = sem("turn_hi")
        turn_free = sem("turn_free")
        ctx_filled = sem("ctx_filled")
        ctx_free = [sem(f"ctx_free{r}") for r in range(ROWS)]
        var_ready = sem("var_ready")
        pow_done = sem("pow_done")
        rs_ready = sem("rs_ready")
        z_ready = [sem(f"z_ready{r}") for r in range(ROWS)]
        y_ready = [sem(f"y_ready{s}") for s in per]
        y_stored = [sem(f"y_stored{s}") for s in per]
        dve_step = sem("dve_step")

        block = ctx.enter_context(nc.Block())

        def nth(item):
            return 2 * item[1] + item[2]

        def released(engine, i, item, g):
            k = GEMM_AT[item] + g
            engine.wait_ge(gemm_free[k % GEMM_BANKS], i * BANK_N + k // GEMM_BANKS + 1)

        def apart(engine):
            engine.sem_inc(waited, 1)

        def plain(layer):
            return layer in (1, 3, -1)

        @block.sync
        def _(sp):
            def load_x(s, i):
                sp.dma_start(x_in[s][:, :, :], x_d[i, s].rearrange("r p d -> p r d")).then_inc(x_loaded[s], 16)

            def load_adj(s, i):
                a, t = (m[i, s].rearrange("r p j -> p r j") for m in (adj_d, adjT_d))
                sp.dma_start(adj[s][:, :, :], a).then_inc(adj_loaded[s], 16)
                sp.dma_start(adjT[s][:, :, :], t).then_inc(adj_loaded[s], 16)
                sp.dma_start(sym[s][:, :, :], t).then_inc(adj_loaded[s], 16)

            for s in per:
                load_x(s, 0)
            sp.dma_start(bias_f[0:NBIAS, :], bias_d).then_inc(const_loaded, 16)
            sp.dma_start(bias_f[NBIAS:2 * NBIAS, :], bias_d).then_inc(const_loaded, 16)
            sp.dma_start(ln_cols[:, :, :, :], lncol_d).then_inc(const_loaded, 16)
            sp.dma_start(ln_rows[:, :, :, :], lnrow_d.partition_broadcast(P)).then_inc(const_loaded, 16)
            for w in range(NW):
                if w >= 2:
                    sp.wait_ge(w_ready, w - 1)
                stage = arena[:, 2 * (w % 2):2 * (w % 2) + 2, :].rearrange("p a n -> p (a n)")[:, 0:KC * D]
                sp.dma_start(stage.rearrange("p (k d) -> p k d", k=KC),
                             w_d[w].rearrange("(k p) d -> p k d", p=P)).then_inc(w_loaded[w % 2], 16)

            def pair(i, last):
                for s in per:
                    sp.wait_ge(adj_used[s], 2 * i)
                    load_adj(s, i)
                if not last:
                    for s in per:
                        sp.wait_ge(resid_used[s], i + 1)
                        load_x(s, i + 1)

            with sp.Fori(0, PAIRS - 1) as i:
                pair(i, False)
            pair(PAIRS - 1, True)

        @block.tensor
        def _(pe):
            def product(out, terms):
                n = sum(3 if len(t) == 4 else 1 for t in terms)
                done = 0
                for t in terms:
                    if len(t) == 4:
                        s_hi, s_lo, m_hi, m_lo = t
                        passes = ((s_hi, m_hi), (s_hi, m_lo), (s_lo, m_hi))
                    else:
                        passes = (t,)
                    for st, mv in passes:
                        ins = nc.tensor.matmul(out, st, mv, start=(done == 0), stop=(done == n - 1))
                        done += 1
                return ins

            def weight(w, k, cols):
                return w_hi[:, w, k, cols], w_lo[:, w, k, cols]

            def features(s, k, rows):
                return hT[s][:, 0, k, rows], hT[s][:, 1, k, rows]

            def tile(r):
                return slice(r * P, (r + 1) * P)

            def bank(i, item, g):
                k = GEMM_AT[item] + g
                pe.wait_ge(gemm_free[k % GEMM_BANKS], i * BANK_N + k // GEMM_BANKS)
                return gemm_ps[k % GEMM_BANKS]

            def project(i, item):
                _, l, s = item
                pe.wait_ge(turn_free, i * TURN_N + turned(item))
                for g in range(3):
                    out = bank(i, item, g)
                    for half in range(2):
                        side, o = divmod(2 * g + half, KC)
                        w = 3 * l + side
                        last = product(out[:, half * S:(half + 1) * S],
                                       [weight(w, k, tile(o)) + features(s, k, slice(0, S)) for k in range(KC)])
                    last.then_inc(gemm_filled, 1)

            def turned(item):
                _, l, s = item
                return s + 1 if l == 0 else 2 + TURN_AT[(TURN, l - 1, s)] + 1

            def values(i, item, w, bias):
                _, l, s = item
                pe.wait_ge(turn_free, i * TURN_N + turned(item))
                for r in range(ROWS):
                    out = bank(i, item, r)
                    product(out[:, 0:D],
                            [features(s, k, tile(r)) + weight(w, k, slice(0, D)) for k in range(KC)]
                            + [(pick[:, bias, :], bias_pair[:, :])]).then_inc(gemm_filled, 1)

            def score_attention(i, item):
                _, l, s = item
                released(pe, i, (PROJECT, l, s), 2)

                def m(side, k, r):
                    at = slice((side * KC + k) * S + r * P, (side * KC + k) * S + (r + 1) * P)
                    return proj[:, 0, at], proj[:, 1, at]

                out = bank(i, item, 0)
                for r in range(ROWS):
                    last = product(out[:, tile(r)], [m(r, k, r) + features(s, k, tile(r)) for k in range(KC)])
                last.then_inc(gemm_filled, 1)
                out = bank(i, item, 1)
                for r in range(ROWS):
                    last = product(out[:, r * S:(r + 1) * S],
                                   [m(1 - r, k, r) + features(s, k, slice(0, S)) for k in range(KC)])
                last.then_inc(gemm_filled, 1)

            def score_convolution(i, item):
                _, l, s = item
                pe.wait_ge(turn_free, i * TURN_N + turned(item))
                out = bank(i, item, 0)
                for r in range(ROWS):
                    last = product(out[:, r * S:(r + 1) * S],
                                   [features(s, k, tile(r)) + features(s, k, slice(0, S)) for k in range(KC)])
                last.then_inc(gemm_filled, 1)

            def turn_probs(i, item):
                _, l, s = item
                n = 2 * (l - 2) + s
                pe.wait_ge(probs_ready, i * 4 + n + 1)
                pe.wait_ge(turn_free, i * TURN_N + 2 + TURN_AT[item])
                for b in range(6):
                    last = nc.tensor.transpose(turn_out(b), work[s][:, tile(b)], ident[:, :])
                last.then_inc(turn_filled, 1)

            def turn_out(b):
                return turn_ps[:, b * P:(b + 1) * P]

            def turn(i, item, k):
                _, l, s = item
                src = {-1: x_in, 0: z, 1: x_mid, 2: z, 3: x_in}[l][s]
                if l == 3:
                    pe.wait_ge(x_loaded[s], 16 * (i + 2))
                elif l == -1:
                    pe.wait_ge(x_loaded[s], 16)
                else:
                    for r in range(ROWS):
                        pe.wait_ge(z_ready[r], i * 6 + 2 * l + s + 1)
                pe.wait_ge(turn_free, k)
                for c in range(KC):
                    for r in range(ROWS):
                        last = nc.tensor.transpose(turn_ps[:, c * S + r * P:c * S + (r + 1) * P],
                                                   src[:, r, tile(c)], ident[:, :])
                last.then_inc(turn_filled, 1)

            def context(i, item):
                _, l, s = item
                n = nth(item)
                if l < 2:
                    pe.wait_ge(probsT_ready, i * 4 + n + 1)
                    released(pe, i, (VALUE, l, s), 1)
                else:
                    pe.wait_ge(turn_free, i * TURN_N + 2 + TURN_AT[(TURN_PROBS, l, s)] + 1)
                    released(pe, i, (LEFT, l, s), 1)
                    released(pe, i, (RIGHT, l, s), 1)
                for r in range(ROWS):
                    if n in (1, 2):
                        pe.wait_ge(z_ready[r], i * 6 + n)
                    else:
                        pe.wait_ge(ctx_free[r], i * 6 + max(n - 2, 0))

                    def pT(block):
                        return probsT[:, 0, tile(block)], probsT[:, 1, tile(block)]

                    def v(buf, j):
                        return buf[:, 0, j, :], buf[:, 1, j, :]
                    if l < 2:
                        terms = [pT(2 * j + r) + v(val[s], j) for j in range(ROWS)]
                    else:
                        lower, upper, other = (3 * r + b for b in range(3))
                        terms = [pT(lower) + v(val_r, r), pT(upper) + v(val[s], r),
                                 pT(other) + v(val[s] if r == 0 else val_r, 1 - r)]
                    product(ctx_ps[:, r, 0:VW], terms).then_inc(ctx_filled, 1)

            pe.wait_ge(pool_const, 1)
            for s in per:
                turn(0, (TURN, -1, s), s)

            def pair(i, last):
                for item in ORDER:
                    stage, l, s = item
                    if l < 2 or stage in (LEFT, SELF, RIGHT):
                        if stage in (PROJECT, VALUE, LEFT, SELF, RIGHT) and s == 0:
                            pe.wait_ge(w_ready, WEIGHTS_BY[(stage, l)])
                            pe.wait_ge(bias_ready, 1)
                    if stage == PROJECT:
                        project(i, item)
                    elif stage == VALUE:
                        values(i, item, 3 * l + 2, l)
                    elif stage == LEFT:
                        values(i, item, 3 * l, 3 * l - 4)
                    elif stage == SELF:
                        values(i, item, 3 * l + 1, 3 * l - 3)
                    elif stage == RIGHT:
                        values(i, item, 3 * l + 2, 3 * l - 2)
                    elif stage == SCORE:
                        (score_attention if l < 2 else score_convolution)(i, item)
                    elif stage == TURN_PROBS:
                        turn_probs(i, item)
                    elif stage == CONTEXT:
                        context(i, item)
                    elif not (last and l == 3):
                        turn(i, item, i * TURN_N + 2 + TURN_AT[item])

            with pe.Fori(0, PAIRS - 1) as i:
                pair(i, False)
            pair(PAIRS - 1, True)

        @block.scalar
        def _(act):
            for w in range(NW):
                stage = arena[:, 2 * (w % 2):2 * (w % 2) + 2, :].rearrange("p a n -> p (a n)")[:, 0:KC * D]
                act.wait_ge(w_loaded[w % 2], 16 * (w // 2 + 1))
                nc.scalar.copy(w_hi[:, w, :, :].rearrange("p k d -> p (k d)"), stage).then_inc(w_hi_done, 1)

            def split_hi(i, item, dst, width=BANK):
                for g in range(groups(item[0], item[1])):
                    k = GEMM_AT[item] + g
                    act.wait_ge(gemm_filled, i * GEMM_N + k + 1)
                    nc.scalar.copy(dst(g), gemm_ps[k % GEMM_BANKS][:, 0:width]).then_inc(hi_done, 1)

            def turn(l, s, k):
                act.wait_ge(turn_filled, k + 1)
                if plain(l):
                    nc.scalar.copy(hT[s][:, 0, :, :].rearrange("p k r -> p (k r)"),
                                   turn_ps[:, 0:KC * S]).then_inc(turn_hi, 1)
                else:
                    for c in range(KC):
                        last = nc.scalar.activation(work[s][:, c * S:(c + 1) * S], turn_ps[:, c * S:(c + 1) * S],
                                                    ACT.Relu, scale=ln_cols[:, l // 2, 0, c:c + 1],
                                                    bias=ln_cols[:, l // 2, 1, c:c + 1])
                    last.then_inc(turn_hi, 1)

            act.wait_ge(const_loaded, 64)
            for s in per:
                turn(-1, s, s)

            def pair(i, last):
                for item in ORDER:
                    stage, l, s = item
                    n = nth(item)
                    if stage == PROJECT:
                        split_hi(i, item, lambda g: proj[:, 0, g * BANK:(g + 1) * BANK])
                    elif stage in (VALUE, LEFT):
                        split_hi(i, item, lambda g: val[s][:, 0, g, 0:D], D)
                    elif stage == RIGHT:
                        split_hi(i, item, lambda g: val_r[:, 0, g, 0:D], D)
                    elif stage == SCORE and l < 2:
                        released(act, i, item, 1)
                        flat = scores[:, :, :].rearrange("p r j -> p (r j)")
                        nc.scalar.activation(flat, flat, ACT.Exp, scale=SCALE).then_inc(exp_done, 1)
                    elif stage == SCORE:
                        k = GEMM_AT[item]
                        act.wait_ge(max_ready, i * 4 + n - 4 + 1)
                        bank = gemm_ps[k % GEMM_BANKS]
                        for r in range(ROWS):
                            last_exp = nc.scalar.activation(scores[:, r, :], bank[:, r * S:(r + 1) * S],
                                                            ACT.Exp, scale=SCALE, bias=col(s, NMAX + r, 1),
                                                            accum_out=col(s, Z + r, 1))
                        last_exp.then_inc(gemm_free[k % GEMM_BANKS], 1)
                    elif stage == TURN_PROBS:
                        act.wait_ge(turn_filled, i * TURN_N + 2 + TURN_AT[item] + 1)
                        nc.scalar.copy(probsT[:, 0, :], turn_ps[:, 0:6 * P]).then_inc(turn_hi, 1)
                    elif stage == CONTEXT and l == 0:
                        act.wait_ge(rs_ready, i * 2 + s + 1)
                        nc.scalar.activation(z[s][:, 0, :], ctx_ps[:, 0, 0:D], ACT.Identity,
                                             scale=col(s, RS, 1), bias=col(s, NB, 1)).then_inc(z_ready[0], 1)
                    elif stage == TURN and not (last and l == 3):
                        turn(l, s, i * TURN_N + 2 + TURN_AT[item])

            with act.Fori(0, PAIRS - 1) as i:
                pair(i, False)
            pair(PAIRS - 1, True)

        @block.vector
        def _(dve):
            base = [0, 0]

            def step(ins):
                ins.then_inc(dve_step, 1)
                base[1] += 1
                return ins

            def settle():
                dve.wait_ge(dve_step, base[0] + base[1])

            vec = nc.vector
            step(vec.memset(exps[:, 0, :], 0.5))
            step(vec.memset(exps[:, 1, :], -0.5))
            for s in per:
                vec.memset(val[s][:, 0, :, D:VW].bitcast(F32), 1.0)
                vec.memset(val[s][:, 1, :, D:VW].bitcast(F32), 0.0)
            dve.wait_ge(const_loaded, 64)
            step(vec.tensor_scalar(bias_neg[:, :], bias_f[:, :], -1.0, None, ALU.mult))
            dve.wait_ge(pool_const, 1)
            settle()
            vec.tensor_copy(pick[:, :, :], pick_f[:, :].unsqueeze(2).to_broadcast([2 * NBIAS, NBIAS, P]))
            vec.scalar_tensor_tensor(bias_pair[:, :], bias_neg[:, :], half_sel[:, :], bias_f[:, :],
                                     ALU.mult, ALU.add).then_inc(bias_ready, 1)
            for w in range(NW):
                stage = arena[:, 2 * (w % 2):2 * (w % 2) + 2, :].rearrange("p a n -> p (a n)")[:, 0:KC * D]
                dve.wait_ge(w_hi_done, w + 1)
                vec.tensor_tensor(w_lo[:, w, :, :].rearrange("p k d -> p (k d)"), stage,
                                  w_hi[:, w, :, :].rearrange("p k d -> p (k d)"), ALU.subtract).then_inc(w_ready, 1)

            def split_lo(i, item, hi, lo, width=BANK):
                for g in range(groups(item[0], item[1])):
                    k = GEMM_AT[item] + g
                    dve.wait_ge(hi_done, i * HI_N + HI_AT[item] + g + 1)
                    vec.tensor_tensor(lo(g), gemm_ps[k % GEMM_BANKS][:, 0:width], hi(g), ALU.subtract)\
                       .then_inc(gemm_free[k % GEMM_BANKS], 1)

            def turn(l, s, k):
                dve.wait_ge(turn_hi, k + 1)
                hi = hT[s][:, 0, :, :].rearrange("p k r -> p (k r)")
                lo = hT[s][:, 1, :, :].rearrange("p k r -> p (k r)")
                if plain(l):
                    vec.tensor_tensor(lo, turn_ps[:, 0:KC * S], hi, ALU.subtract).then_inc(turn_free, 1)
                else:
                    step(vec.tensor_copy(hi, work[s]))
                    settle()
                    vec.tensor_tensor(lo, work[s], hi, ALU.subtract).then_inc(turn_free, 1)

            def blocks_flat(t):
                return t.rearrange("p r j -> p (r j)")

            def score_attention(i, item):
                _, l, s = item
                n = nth(item)
                k = GEMM_AT[item]
                other, own = gemm_ps[k % GEMM_BANKS], gemm_ps[(k + 1) % GEMM_BANKS]
                if l == 0:
                    dve.wait_ge(adj_loaded[s], 48 * (i + 1))
                    apart(dve)
                    step(vec.copy_predicated(blocks_flat(sym[s]), blocks_flat(from_adj), blocks_flat(adj[s])))
                dve.wait_ge(gemm_filled, i * GEMM_N + k + 2)
                apart(dve)
                diag = own[:, :].rearrange("p (a j) -> p a j", j=P)[:, 0:4:3, :]
                vec.copy_predicated(diag, take_side[:, :, :], other[:, 0:ROWS * P].rearrange("p (a j) -> p a j", j=P))\
                   .then_inc(gemm_free[k % GEMM_BANKS], 1)
                released(dve, i, item, 0)
                settle()
                vec.tensor_tensor(blocks_flat(scores), own[:, :], blocks_flat(sym[s]), ALU.mult)\
                   .then_inc(gemm_free[(k + 1) % GEMM_BANKS], 1)
                dve.wait_ge(exp_done, i * 4 + n + 1)
                step(vec.tensor_tensor(blocks_flat(scores), blocks_flat(scores), blocks_flat(adjT[s]), ALU.mult))
                settle()
                hi, lo = probsT[:, 0, 0:4 * P], probsT[:, 1, 0:4 * P]
                vec.tensor_copy(hi, blocks_flat(scores)).then_inc(adjT_used[s], 1)
                dve.wait_ge(adjT_used[s], i * 2 + l + 1)
                vec.tensor_tensor(lo, blocks_flat(scores), hi, ALU.subtract).then_inc(probsT_ready, 1)

            def row_max(i, item):
                _, l, s = item
                k = GEMM_AT[item]
                if l == 2:
                    for r in range(ROWS):
                        step(vec.scalar_tensor_tensor(junk[:, r, :], adj[s][:, r, r * P:(r + 1) * P], 1.0, ident[:, :],
                                                      ALU.mult, ALU.mult, accum_out=col(s, ADIAG + r, 1)))
                dve.wait_ge(gemm_filled, i * GEMM_N + k + 1)
                step(vec.tensor_reduce(col(s, MAXV), gemm_ps[k % GEMM_BANKS][:, :].rearrange("p (r j) -> p r j", r=ROWS),
                                       AX.X, ALU.max))
                settle()
                vec.tensor_scalar(col(s, NMAX), col(s, MAXV), -SCALE, None, ALU.mult).then_inc(max_ready, 1)

            def mask_probs(i, l, s):
                released(dve, i, (SCORE, l, s), 0)
                dve.wait_ge(tri_ready[s], i + 1)
                p = work[s].rearrange("p (r b j) -> p r b j", r=ROWS, b=3)
                e = scores[:, :, :]
                for r in range(ROWS):
                    e_diag = e[:, r, r * P:(r + 1) * P]
                    step(vec.scalar_tensor_tensor(junk[:, r, :], e_diag, 1.0, ident[:, :], ALU.mult, ALU.mult,
                                                  accum_out=col(s, PDIAG + r, 1)))
                    tri = adjT[s][:, r, :].rearrange("p (b j) -> p b j", b=2)
                    vec.tensor_tensor(p[:, r, 0:2, :], e_diag.unsqueeze(1).to_broadcast([P, 2, P]), tri, ALU.mult)
                flat_e, flat_a = blocks_flat(scores), blocks_flat(adj[s])
                vec.tensor_tensor(p[:, :, 2, :], flat_e[:, P:3 * P].rearrange("p (r j) -> p r j", r=ROWS),
                                  flat_a[:, P:3 * P].rearrange("p (r j) -> p r j", r=ROWS), ALU.mult)\
                   .then_inc(probs_ready, 1)
                settle()
                vec.tensor_tensor(col(s, PDIAG), col(s, PDIAG), col(s, ADIAG), ALU.mult).then_inc(adj_used[s], 1)
                dve.wait_ge(adj_used[s], i * 2 + l - 1)
                step(vec.scalar_tensor_tensor(col(s, QSUM), col(s, Z), 1e-10, col(s, PDIAG), ALU.mult, ALU.add))

            def mean_var(s, src, ready=dve_step):
                for r in range(ROWS):
                    step(vec.bn_stats(stats(s, r), src(r)))
                settle()
                apart(dve)
                for r in range(ROWS):
                    ins = vec.bn_aggr(small[s][:, MV + 2 * r:MV + 2 * r + 2], stats(s, r))
                    if ready is dve_step or r == 0:
                        step(ins)
                    else:
                        ins.then_inc(ready, 1)

            def outer_norm(i, item, dst):
                _, l, s = item
                mean_var(s, lambda r: z[s][:, r, :])
                settle()
                vec.tensor_scalar(col(s, VARP), variances(s), 1e-5, None, ALU.add).then_inc(var_ready, 1)
                dve.wait_ge(pow_done, i * POW_N + POW_AT[item] + 2)
                for r in range(ROWS):
                    last = vec.tensor_scalar(dst[:, r, :], z[s][:, r, :], mean(s, r), col(s, ROOT + r, 1),
                                             ALU.subtract, ALU.mult)
                    if l == 1:
                        last.then_inc(z_ready[r], 1)
                if l == 3:
                    last.then_inc(y_ready[s], 1)

            def context_read(i, item):
                for r in range(ROWS):
                    dve.wait_ge(ctx_free[r], i * 6 + nth(item) - 1)

            def relu_residual(i, item, resid, src):
                _, l, s = item
                for r in range(ROWS):
                    ins = vec.scalar_tensor_tensor(z[s][:, r, :], src(r), mean(s, r), ln_rows[:, l // 2, 0, :],
                                                   ALU.subtract, ALU.mult)
                    if l == 1:
                        ins.then_inc(ctx_free[r], 1)
                    else:
                        step(ins)
                if l == 1:
                    context_read(i, item)
                settle()
                for r in range(ROWS):
                    step(vec.scalar_tensor_tensor(z[s][:, r, :], z[s][:, r, :], col(s, RS + r, 1), ln_rows[:, l // 2, 1, :],
                                                  ALU.mult, ALU.add))
                settle()
                for r in range(ROWS):
                    ins = vec.scalar_tensor_tensor(z[s][:, r, :], z[s][:, r, :], 0.0, resid[:, r, :],
                                                   ALU.max, ALU.add)
                    if l == 1 and r == ROWS - 1:
                        ins.then_inc(resid_used[s], 1)
                    else:
                        step(ins)
                if l == 1:
                    dve.wait_ge(resid_used[s], i + 1)
                settle()

            def context_attention(i, item):
                _, l, s = item
                dve.wait_ge(ctx_filled, i * 16 + 2 * nth(item) + 2)
                mean_var(s, lambda r: ctx_ps[:, r, 0:D], var_ready)
                step(vec.tensor_scalar(col(s, EPS), row_sums, 1e-3, 1e-13, ALU.mult, ALU.add))
                dve.wait_ge(pow_done, i * POW_N + POW_AT[item] + 1)
                settle()
                step(vec.scalar_tensor_tensor(col(s, DEN), col(s, ROOT), (D / (D - 1.0)) ** 0.5, col(s, EPS),
                                              ALU.mult, ALU.add))
                settle()
                step(vec.reciprocal(col(s, RS), col(s, DEN)))
                settle()
                if l == 0:
                    dve.wait_ge(y_stored[s], 16 * i)
                    vec.scalar_tensor_tensor(col(s, NB), means(s), -1.0, col(s, RS), ALU.mult, ALU.mult)\
                       .then_inc(rs_ready, 1)
                    vec.tensor_scalar(z[s][:, 1, :], ctx_ps[:, 1, 0:D], mean(s, 1), col(s, RS + 1, 1),
                                      ALU.subtract, ALU.mult).then_inc(z_ready[1], 1)
                else:
                    relu_residual(i, item, x_in[s], lambda r: ctx_ps[:, r, 0:D])
                    outer_norm(i, item, x_mid[s])

            def context_convolution(i, item):
                _, l, s = item
                dve.wait_ge(ctx_filled, i * 16 + 2 * nth(item) + 2)
                step(vec.tensor_tensor(col(s, QSUM), row_sums, col(s, QSUM), ALU.add))
                for r in range(ROWS):
                    released(dve, i, (SELF, l, s), r)
                    vec.scalar_tensor_tensor(z[s][:, r, :], z[s][:, r, :], col(s, PDIAG + r, 1),
                                             ctx_ps[:, r, 0:D], ALU.mult, ALU.add).then_inc(ctx_free[r], 1)
                context_read(i, item)
                settle()
                step(vec.scalar_tensor_tensor(col(s, EPS), col(s, QSUM), 1e-12, col(s, QSUM), ALU.mult, ALU.mult))
                mean_var(s, lambda r: z[s][:, r, :])
                settle()
                vec.tensor_tensor(col(s, VARP), variances(s), col(s, EPS), ALU.add).then_inc(var_ready, 1)
                dve.wait_ge(pow_done, i * POW_N + POW_AT[item] + 1)
                if l == 2:
                    for r in range(ROWS):
                        vec.tensor_scalar(z[s][:, r, :], z[s][:, r, :], mean(s, r), col(s, RS + r, 1),
                                          ALU.subtract, ALU.mult).then_inc(z_ready[r], 1)
                else:
                    relu_residual(i, item, x_mid[s], lambda r: z[s][:, r, :])
                    outer_norm(i, item, z[s])

            for s in per:
                turn(-1, s, s)

            def pair(i, last):
                base[0] = i * DVE_STEPS + start
                base[1] = 0
                for item in ORDER:
                    stage, l, s = item
                    if stage == PROJECT:
                        split_lo(i, item, lambda g: proj[:, 0, g * BANK:(g + 1) * BANK],
                                 lambda g: proj[:, 1, g * BANK:(g + 1) * BANK])
                    elif stage in (VALUE, LEFT):
                        split_lo(i, item, lambda g: val[s][:, 0, g, 0:D], lambda g: val[s][:, 1, g, 0:D], D)
                        if stage == LEFT:
                            mask_probs(i, l, s)
                    elif stage == RIGHT:
                        if l == 2 and s == 0:
                            vec.memset(val_r[:, 0, :, D:VW].bitcast(F32), 1.0)
                            vec.memset(val_r[:, 1, :, D:VW].bitcast(F32), 0.0)
                        split_lo(i, item, lambda g: val_r[:, 0, g, 0:D], lambda g: val_r[:, 1, g, 0:D], D)
                    elif stage == SELF:
                        for g in range(ROWS):
                            k = GEMM_AT[item] + g
                            dve.wait_ge(gemm_filled, i * GEMM_N + k + 1)
                            vec.tensor_copy(z[s][:, g, :], gemm_ps[k % GEMM_BANKS][:, 0:D])\
                               .then_inc(gemm_free[k % GEMM_BANKS], 1)
                    elif stage == SCORE:
                        (score_attention if l < 2 else row_max)(i, item)
                    elif stage == TURN_PROBS:
                        dve.wait_ge(turn_hi, i * TURN_N + 2 + TURN_AT[item] + 1)
                        vec.tensor_tensor(probsT[:, 1, :], turn_ps[:, 0:6 * P], probsT[:, 0, :], ALU.subtract)\
                           .then_inc(turn_free, 1)
                    elif stage == CONTEXT:
                        (context_attention if l < 2 else context_convolution)(i, item)
                    elif not (last and l == 3):
                        turn(l, s, i * TURN_N + 2 + TURN_AT[item])
                assert base[1] == DVE_STEPS

            start = base[1]
            with dve.Fori(0, PAIRS - 1) as i:
                pair(i, False)
            pair(PAIRS - 1, True)

        @block.gpsimd
        def _(pool):
            gp = nc.gpsimd
            gp.memset(ident[:, :], 0.0).then_inc(pool_step, 1)
            gp.memset(half_sel[:, :], 1.0).then_inc(pool_step, 1)
            gp.memset(pick_f[:, :], 0.0).then_inc(pool_step, 1)
            gp.memset(from_adj[:, :, :], 1.0).then_inc(pool_step, 1)
            gp.memset(take_side[:, :, :], 1.0).then_inc(pool_step, 1)
            pool.wait_ge(pool_step, 5)
            gp.affine_select(out=ident[:, :], in_=ident[:, :], compare_op=ALU.not_equal, fill=1.0, base=0,
                             pattern=[[-1, P]], channel_multiplier=1)
            gp.affine_select(out=half_sel[:, :], in_=half_sel[:, :], compare_op=ALU.is_ge, fill=0.0, base=-NBIAS,
                             pattern=[[0, 1]], channel_multiplier=1)
            gp.affine_select(out=pick_f[:, :], in_=pick_f[:, :], compare_op=ALU.not_equal, fill=1.0, base=0,
                             pattern=[[-1, NBIAS]], channel_multiplier=1).then_inc(pool_step, 1)
            pool.wait_ge(pool_step, 6)
            gp.affine_select(out=pick_f[:, :], in_=pick_f[:, :], compare_op=ALU.not_equal, fill=1.0, base=-NBIAS,
                             pattern=[[-1, NBIAS]], channel_multiplier=1)
            gp.affine_select(out=from_adj[:, :, :], in_=from_adj[:, :, :], compare_op=ALU.is_gt, fill=0.0, base=0,
                             pattern=[[-P, ROWS], [1, S]], channel_multiplier=-1)
            gp.affine_select(out=take_side[:, 0, :], in_=take_side[:, 0, :], compare_op=ALU.is_ge, fill=0.0, base=0,
                             pattern=[[-1, P]], channel_multiplier=1)
            gp.affine_select(out=take_side[:, 1, :], in_=take_side[:, 1, :], compare_op=ALU.is_gt, fill=0.0, base=0,
                             pattern=[[1, P]], channel_multiplier=-1).then_inc(pool_const, 1)

            def power(i, item, second=False):
                _, l, s = item
                pool.wait_ge(var_ready, i * POW_N + POW_AT[item] + 1 + second)
                if second:
                    gp.tensor_tensor(col(s, ROOT), col(s, VARP), exps[:, 1, :], ALU.pow).then_inc(pow_done, 1)
                elif l < 2:
                    gp.tensor_tensor(col(s, ROOT), variances(s), exps[:, 0, :], ALU.pow).then_inc(pow_done, 1)
                else:
                    gp.tensor_tensor(col(s, RS), col(s, VARP), exps[:, 1, :], ALU.pow).then_inc(pow_done, 1)

            def pair(i):
                for item in ORDER:
                    stage, l, s = item
                    if stage == CONTEXT:
                        power(i, item)
                        if l % 2:
                            power(i, item, True)
                        if l == 3:
                            pool.wait_ge(y_ready[s], i + 1)
                            gp.dma_start(out_d[i, s].rearrange("r p d -> p r d"), z[s][:, :, :]).then_inc(y_stored[s], 16)
                    if stage == SCORE and l == 1:
                        pool.wait_ge(adjT_used[s], 2 * i + 2)
                        apart(pool)
                        for r in range(ROWS):
                            a = adj[s][:, r, r * P:(r + 1) * P]
                            gp.affine_select(out=adjT[s][:, r, 0:P], in_=a, compare_op=ALU.is_gt, fill=0.0, base=0,
                                             pattern=[[-1, P]], channel_multiplier=1)
                            tri = gp.affine_select(out=adjT[s][:, r, P:S], in_=a, compare_op=ALU.is_gt, fill=0.0,
                                                   base=0, pattern=[[1, P]], channel_multiplier=-1)
                        tri.then_inc(tri_ready[s], 1)

            with pool.Fori(0, PAIRS) as i:
                pair(i)
            for s in per:
                pool.wait_ge(y_stored[s], 16 * PAIRS)


WEIGHTS_BY = {(PROJECT, 0): 2, (VALUE, 0): 3, (PROJECT, 1): 5, (VALUE, 1): 6,
              (LEFT, 2): 7, (SELF, 2): 8, (RIGHT, 2): 9, (LEFT, 3): 10, (SELF, 3): 11, (RIGHT, 3): 12}


def kernel(x, adj, L0_gnn_W_left, L0_gnn_W_right, L0_gnn_W_lin, L0_gnn_b_lin, L0_gnn_ln_a, L0_gnn_ln_b,
           L1_gnn_Wl, L1_gnn_bl, L1_gnn_Ws, L1_gnn_bs, L1_gnn_Wr, L1_gnn_br, L1_gnn_ln_w, L1_gnn_ln_b):
    import numpy as np
    import concourse.bacc as bacc
    from concourse.bass_utils import run_bass_kernel_spmd

    f = lambda a: np.ascontiguousarray(np.asarray(a))
    t = lambda a: np.swapaxes(np.asarray(a), -1, -2)
    grid = (PAIRS, STREAMS, ROWS, P)
    weights = []
    for l in range(2):
        weights += [t(L0_gnn_W_left[l]), t(L0_gnn_W_right[l]), t(L0_gnn_W_lin[l])]
    for l in range(2):
        weights += [t(L1_gnn_Wl[l]), t(L1_gnn_Ws[l]), t(L1_gnn_Wr[l])]
    biases = [L0_gnn_b_lin[0], L0_gnn_b_lin[1]]
    for l in range(2):
        biases += [L1_gnn_bl[l], L1_gnn_bs[l], L1_gnn_br[l]]
    cols = [[L0_gnn_ln_a[0], L0_gnn_ln_b[0]], [L1_gnn_ln_w[0], L1_gnn_ln_b[0]]]
    rows = [[L0_gnn_ln_a[1], L0_gnn_ln_b[1]], [L1_gnn_ln_w[1], L1_gnn_ln_b[1]]]
    arrays = {
        "x_dram": f(x).reshape(grid + (D,)),
        "adj_dram": f(adj).reshape(grid + (S,)),
        "adjT_dram": f(t(adj)).reshape(grid + (S,)),
        "w_dram": f(np.stack([np.asarray(w) for w in weights])),
        "bias_dram": f(np.stack([np.asarray(b) for b in biases])),
        "lncol_dram": f(np.asarray(np.stack([[np.asarray(c) for c in p] for p in cols])).reshape(2, 2, KC, P).transpose(3, 0, 1, 2)),
        "lnrow_dram": f(np.stack([[np.asarray(c) for c in p] for p in rows])),
    }
    nc = bacc.Bacc("TRN2", target_bir_lowering=False, num_devices=1)
    args = [nc.dram_tensor(n, a.shape, mybir.dt.from_np(a.dtype), kind="ExternalInput").ap() for n, a in arrays.items()]
    out = nc.dram_tensor("out_dram", grid + (D,), F32, kind="ExternalOutput").ap()
    build(nc, *args, out)
    r = run_bass_kernel_spmd(nc, [arrays], core_ids=[0])
    return r.results[0]["out_dram"].reshape(B, S, D)
```

```python
import concourse.bass as bass
from concourse import mybir
from contextlib import ExitStack

F32 = mybir.dt.float32
F32R = mybir.dt.float32r
I8 = mybir.dt.int8
ALU = mybir.AluOpType
ACT = mybir.ActivationFunctionType
AX = mybir.AxisListType

P = 128
B, S, D = 32, 256, 384
ROWS = S // P
KC = D // P
STREAMS = 2
PAIRS = B // STREAMS
LAYERS = 4
VW = D + 2
SCALE = 1.0 / float(D) ** 0.5
GEMM_BANKS = 4
BANK = 512

PROJECT, VALUE, OTHER, SCORE = "project", "value", "score_other_side", "score"
LEFT, SELF, RIGHT = "value_left", "value_self", "value_right"
GEMMS = (PROJECT, VALUE, OTHER, SCORE, LEFT, SELF, RIGHT)
TURN, TURN_PROBS, CONTEXT, MASK, NORM, FINISH = "turn", "turn_probs", "context", "mask", "norm", "finish"


def order():
    out = []
    for l in range(LAYERS):
        for s in range(STREAMS):
            other = 1 - s
            due = l - 1 if s == 0 else l
            context, norm, finish = (CONTEXT, due, other, 0), (NORM, due, other, 0), (FINISH, due, other, 0)
            turn = (TURN, due % LAYERS - LAYERS if due in (-1, LAYERS - 1) else due, other, 0)
            ends = [finish] if due % 2 else []
            if l == 0 and s == 0:
                out += [(TURN, -1, 0, 0), CARRIED[0], (PROJECT, 0, 0, 0), CARRIED[1], (PROJECT, 0, 0, 1),
                        (PROJECT, 0, 0, 2), CARRIED[2], (VALUE, 0, 0, 0), (TURN, -1, 1, 0), (VALUE, 0, 0, 1),
                        (OTHER, 0, 0, 0), (SCORE, 0, 0, 0)]
            elif l < 2 and due == 1:
                out += [(PROJECT, l, s, 0), (PROJECT, l, s, 1), context, (PROJECT, l, s, 2), norm, (VALUE, l, s, 0),
                        finish, (VALUE, l, s, 1), (OTHER, l, s, 0), turn, (SCORE, l, s, 0)]
            elif l < 2:
                out += [(PROJECT, l, s, 0), (PROJECT, l, s, 1), context, (PROJECT, l, s, 2), norm, (VALUE, l, s, 0),
                        (VALUE, l, s, 1), turn, (OTHER, l, s, 0), (SCORE, l, s, 0)]
            elif due == 1:
                out += [(SCORE, l, s, 0), (MASK, l, s, 0), (LEFT, l, s, 0), context, (LEFT, l, s, 1), norm,
                        (SELF, l, s, 0), (TURN_PROBS, l, s, 0), finish, (SELF, l, s, 1), (RIGHT, l, s, 0),
                        (RIGHT, l, s, 1), turn, (CONTEXT, l, s, 0)]
            else:
                early = l == 2 and s == 1
                out += [(SCORE, l, s, 0), (MASK, l, s, 0)] + ([] if early else [context])
                out += [(LEFT, l, s, 0), norm, (LEFT, l, s, 1), (SELF, l, s, 0), (TURN_PROBS, l, s, 0), (SELF, l, s, 1)]
                out += ends if due == 3 else [turn]
                out += [(RIGHT, l, s, 0), (RIGHT, l, s, 1)]
    return out


CARRIED = [(CONTEXT, LAYERS - 1, 1, 0), (NORM, LAYERS - 1, 1, 0), (FINISH, LAYERS - 1, 1, 0)]
ORDER = order()


def ordinals(kinds, weight=lambda layer: 1):
    at, n = {}, 0
    for item in ORDER:
        if item[0] in kinds and item not in CARRIED:
            at[item] = n
            n += weight(item[1])
    for item in CARRIED:
        if item[0] in kinds:
            at[item] = n
            n += weight(item[1])
    return at, n


GEMM_AT, GEMM_N = ordinals(GEMMS)
HI_AT, HI_N = ordinals((PROJECT, VALUE, LEFT, RIGHT))
TURN_AT, TURN_N = ordinals((TURN, TURN_PROBS))
POW_AT, POW_N = ordinals((CONTEXT, FINISH))
STEPS = {(SCORE, 0): 2, (SCORE, 1): 1, (SCORE, 2): 3, (SCORE, 3): 1, (MASK, 2): 3, (MASK, 3): 3,
         (CONTEXT, 0): 4, (CONTEXT, 1): 4, (CONTEXT, 2): 6, (CONTEXT, 3): 6,
         (NORM, 0): 2, (NORM, 1): 9, (NORM, 3): 10}
DVE_STEPS = sum(STEPS.get(item[:2], 0) for item in ORDER)
CARRIED_STEPS = sum(STEPS.get(item[:2], 0) for item in CARRIED)
assert GEMM_N % GEMM_BANKS == 0
BANK_N = GEMM_N // GEMM_BANKS


def build(nc, x_d, adj_d, adjT_d, w_d, bias_d, lncol_d, lnrow_d, out_d):
    ctx = ExitStack()
    with ctx:
        def sb(name, shape, dt=F32):
            return ctx.enter_context(nc.sbuf_tensor(name, shape, dt))

        def ps(name, shape):
            return ctx.enter_context(nc.psum_tensor(name, shape, F32))

        def sem(name):
            return ctx.enter_context(nc.semaphore(name))

        NW = 12
        w_hi = sb("w_hi", [P, NW, KC, D], F32R)
        w_lo = sb("w_lo", [P, NW, KC, D], F32R)
        NBIAS = 8
        bias_f = sb("bias_f", [2 * NBIAS, D])
        bias_pair = sb("bias_pair", [2 * NBIAS, D], F32R)
        bias_neg = sb("bias_neg", [2 * NBIAS, D], F32R)
        pick = sb("pick", [2 * NBIAS, NBIAS, P], F32R)
        pick_f = sb("pick_f", [2 * NBIAS, NBIAS])
        half_sel = sb("half_sel", [2 * NBIAS, 1])
        ln_rows = sb("ln_rows", [P, 2, 2, D])
        ln_cols = sb("ln_cols", [P, 2, 2, KC])
        ident = sb("ident", [P, P])
        from_adj = sb("from_adj", [P, ROWS, S], I8)
        take_side = sb("take_side", [P, ROWS, P], I8)
        exps = sb("exps", [P, 2, 2])

        proj = sb("proj", [P, 2, 6 * S + 8], F32R)
        scores = sb("scores", [P, ROWS, S])
        probsT = sb("probsT", [P, 2, 6 * P], F32R)

        per = range(STREAMS)
        arena = sb("arena", [P, 2 * STREAMS, ROWS * D])
        z = [arena[:, s, :].rearrange("p (r d) -> p r d", r=ROWS) for s in per]
        work = [arena[:, STREAMS + s, :] for s in per]
        hT = [sb(f"hT{s}", [P, 2, KC, S], F32R) for s in per]
        val = [sb(f"val{s}", [P, 2, ROWS, VW], F32R) for s in per]
        adj = [sb(f"adj{s}", [P, ROWS, S]) for s in per]
        adjT = [sb(f"adjT{s}", [P, ROWS, S]) for s in per]
        sym = [sb(f"sym{s}", [P, ROWS, S]) for s in per]
        x_in = [sb(f"x_in{s}", [P, ROWS, D]) for s in per]
        x_mid = [sb(f"x_mid{s}", [P, ROWS, D]) for s in per]
        small = [sb(f"small{s}", [P, 64]) for s in per]
        junk = sb("junk", [P, ROWS, P])

        val_r = proj[:, :, 0:ROWS * VW].rearrange("p h (r v) -> p h r v", r=ROWS)

        def col(s, first, n=ROWS):
            return small[s][:, first:first + n]
        STATS, MV, ROOT, RS, NB, EPS, DEN = 0, 12, 16, 18, 20, 22, 24
        ADIAG, PDIAG, Z, NMAX, MAXV, QSUM, VARP = 26, 28, 30, 32, 34, 36, 38

        def stats(s, r):
            return small[s][:, STATS + 6 * r:STATS + 6 * r + 6]

        def mean(s, r):
            return small[s][:, MV + 2 * r:MV + 2 * r + 1]

        def means(s):
            return small[s][:, MV:MV + 4].rearrange("p (r c) -> p r c", c=2)[:, :, 0]

        def variances(s):
            return small[s][:, MV:MV + 4].rearrange("p (r c) -> p r c", c=2)[:, :, 1]

        gemm_ps = [ps(f"gemm_ps{b}", [P, BANK]) for b in range(GEMM_BANKS)]
        turn_ps = ps("turn_ps", [P, 2 * BANK])
        ctx_ps = ps("ctx_ps", [P, ROWS, BANK])
        row_sums = ctx_ps[:, :, D]

        x_loaded = [sem(f"x_loaded{s}") for s in per]
        adj_loaded = [sem(f"adj_loaded{s}") for s in per]
        resid_used = [sem(f"resid_used{s}") for s in per]
        adj_used = [sem(f"adj_used{s}") for s in per]
        adjT_used = [sem(f"adjT_used{s}") for s in per]
        tri_ready = [sem(f"tri_ready{s}") for s in per]
        w_loaded = [sem(f"w_loaded{i}") for i in range(2)]
        w_hi_done = sem("w_hi_done")
        w_ready = sem("w_ready")
        const_loaded = sem("const_loaded")
        pool_const = sem("pool_const")
        pool_step = sem("pool_step")
        waited = sem("waited")
        bias_ready = sem("bias_ready")
        gemm_filled = sem("gemm_filled")
        gemm_free = [sem(f"gemm_free{b}") for b in range(GEMM_BANKS)]
        hi_done = sem("hi_done")
        max_ready = sem("max_ready")
        exp_done = sem("exp_done")
        probs_ready = sem("probs_ready")
        probsT_ready = sem("probsT_ready")
        turn_filled = sem("turn_filled")
        turn_hi = sem("turn_hi")
        relu_done = sem("relu_done")
        turn_free = sem("turn_free")
        ctx_filled = sem("ctx_filled")
        ctx_free = [sem(f"ctx_free{r}") for r in range(ROWS)]
        var_ready = sem("var_ready")
        pow_done = sem("pow_done")
        rs_ready = sem("rs_ready")
        z_ready = [sem(f"z_ready{r}") for r in range(ROWS)]
        y_ready = [sem(f"y_ready{s}") for s in per]
        y_stored = [sem(f"y_stored{s}") for s in per]
        dve_step = sem("dve_step")

        block = ctx.enter_context(nc.Block())

        def nth(item):
            return 2 * item[1] + item[2]

        def released(engine, i, item):
            k = GEMM_AT[item]
            engine.wait_ge(gemm_free[k % GEMM_BANKS], i * BANK_N + k // GEMM_BANKS + 1)

        def apart(engine):
            engine.sem_inc(waited, 1)

        def plain(layer):
            return layer in (-1, 1)

        def run(engine, pair):
            pair(0, [item for item in ORDER if item not in CARRIED])
            with engine.Fori(1, PAIRS) as i:
                pair(i, ORDER)
            pair(PAIRS, CARRIED)

        @block.sync
        def _(sp):
            def load_x(s, i):
                sp.dma_start(x_in[s][:, :, :], x_d[i, s].rearrange("r p d -> p r d")).then_inc(x_loaded[s], 16)

            def load_adj(s, i):
                a, t = (m[i, s].rearrange("r p j -> p r j") for m in (adj_d, adjT_d))
                sp.dma_start(adj[s][:, :, :], a).then_inc(adj_loaded[s], 16)
                sp.dma_start(adjT[s][:, :, :], t).then_inc(adj_loaded[s], 16)
                sp.dma_start(sym[s][:, :, :], t).then_inc(adj_loaded[s], 16)

            for s in per:
                load_x(s, 0)
            sp.dma_start(bias_f[0:NBIAS, :], bias_d).then_inc(const_loaded, 16)
            sp.dma_start(bias_f[NBIAS:2 * NBIAS, :], bias_d).then_inc(const_loaded, 16)
            sp.dma_start(ln_cols[:, :, :, :], lncol_d).then_inc(const_loaded, 16)
            sp.dma_start(ln_rows[:, :, :, :], lnrow_d.partition_broadcast(P)).then_inc(const_loaded, 16)
            for w in range(NW):
                if w >= 2:
                    sp.wait_ge(w_ready, w - 1)
                stage = arena[:, 2 * (w % 2):2 * (w % 2) + 2, :].rearrange("p a n -> p (a n)")[:, 0:KC * D]
                sp.dma_start(stage.rearrange("p (k d) -> p k d", k=KC),
                             w_d[w].rearrange("(k p) d -> p k d", p=P)).then_inc(w_loaded[w % 2], 16)

            for s in per:
                load_adj(s, 0)
            with sp.Fori(1, PAIRS) as i:
                for s in per:
                    sp.wait_ge(resid_used[s], i)
                    load_x(s, i)
                for s in per:
                    sp.wait_ge(adj_used[s], 2 * i)
                    load_adj(s, i)

        @block.tensor
        def _(pe):
            def product(out, terms):
                n = sum(3 if len(t) == 4 else 1 for t in terms)
                done = 0
                for t in terms:
                    if len(t) == 4:
                        s_hi, s_lo, m_hi, m_lo = t
                        passes = ((s_hi, m_hi), (s_hi, m_lo), (s_lo, m_hi))
                    else:
                        passes = (t,)
                    for st, mv in passes:
                        ins = nc.tensor.matmul(out, st, mv, start=(done == 0), stop=(done == n - 1))
                        done += 1
                return ins

            def weight(w, k, cols):
                return w_hi[:, w, k, cols], w_lo[:, w, k, cols]

            def features(s, k, rows):
                return hT[s][:, 0, k, rows], hT[s][:, 1, k, rows]

            def tile(r):
                return slice(r * P, (r + 1) * P)

            def bank(i, item):
                k = GEMM_AT[item]
                pe.wait_ge(gemm_free[k % GEMM_BANKS], i * BANK_N + k // GEMM_BANKS)
                return gemm_ps[k % GEMM_BANKS]

            def featured(i, item):
                _, l, s, _ = item
                pe.wait_ge(turn_free, i * TURN_N + TURN_AT[(TURN, l - 1, s, 0)] + 1)

            def project(i, item):
                _, l, s, g = item
                featured(i, item)
                out = bank(i, item)
                for half in range(2):
                    side, o = divmod(2 * g + half, KC)
                    last = product(out[:, half * S:(half + 1) * S],
                                   [weight(3 * l + side, k, tile(o)) + features(s, k, slice(0, S)) for k in range(KC)])
                last.then_inc(gemm_filled, 1)

            def values(i, item, w, bias):
                _, l, s, r = item
                featured(i, item)
                out = bank(i, item)
                product(out[:, 0:D],
                        [features(s, k, tile(r)) + weight(w, k, slice(0, D)) for k in range(KC)]
                        + [(pick[:, bias, :], bias_pair[:, :])]).then_inc(gemm_filled, 1)

            def projected(side, k, r):
                at = slice((side * KC + k) * S + r * P, (side * KC + k) * S + (r + 1) * P)
                return proj[:, 0, at], proj[:, 1, at]

            def score_other_side(i, item):
                _, l, s, _ = item
                released(pe, i, (PROJECT, l, s, 2))
                out = bank(i, item)
                for r in range(ROWS):
                    last = product(out[:, tile(r)], [projected(r, k, r) + features(s, k, tile(r)) for k in range(KC)])
                last.then_inc(gemm_filled, 1)

            def score_attention(i, item):
                _, l, s, _ = item
                out = bank(i, item)
                for r in range(ROWS):
                    last = product(out[:, r * S:(r + 1) * S],
                                   [projected(1 - r, k, r) + features(s, k, slice(0, S)) for k in range(KC)])
                last.then_inc(gemm_filled, 1)

            def score_convolution(i, item):
                _, l, s, _ = item
                featured(i, item)
                out = bank(i, item)
                for r in range(ROWS):
                    last = product(out[:, r * S:(r + 1) * S],
                                   [features(s, k, tile(r)) + features(s, k, slice(0, S)) for k in range(KC)])
                last.then_inc(gemm_filled, 1)

            def turn_probs(i, item):
                _, l, s, _ = item
                pe.wait_ge(probs_ready, i * 4 + 2 * (l - 2) + s + 1)
                pe.wait_ge(turn_free, i * TURN_N + TURN_AT[item])
                for b in range(6):
                    last = nc.tensor.transpose(turn_out(b), work[s][:, tile(b)], ident[:, :])
                last.then_inc(turn_filled, 1)

            def turn_out(b):
                return turn_ps[:, b * P:(b + 1) * P]

            def turn(i, item):
                _, l, s, _ = item
                src = {-1: x_in, 0: z, 1: x_mid, 2: z}[l][s]
                if l == -1:
                    pe.wait_ge(x_loaded[s], 16 * (i + 1))
                else:
                    for r in range(ROWS):
                        pe.wait_ge(z_ready[r], i * 6 + 2 * l + s + 1)
                pe.wait_ge(turn_free, i * TURN_N + TURN_AT[item])
                for c in range(KC):
                    for r in range(ROWS):
                        last = nc.tensor.transpose(turn_ps[:, c * S + r * P:c * S + (r + 1) * P],
                                                   src[:, r, tile(c)], ident[:, :])
                last.then_inc(turn_filled, 1)

            def context(i, item):
                _, l, s, _ = item
                n = nth(item)
                if l < 2:
                    pe.wait_ge(probsT_ready, i * 4 + n + 1)
                    released(pe, i, (VALUE, l, s, 1))
                else:
                    pe.wait_ge(turn_free, i * TURN_N + TURN_AT[(TURN_PROBS, l, s, 0)] + 1)
                    released(pe, i, (LEFT, l, s, 1))
                    released(pe, i, (RIGHT, l, s, 1))
                for r in range(ROWS):
                    if n in (1, 2):
                        pe.wait_ge(z_ready[r], i * 6 + n)
                    else:
                        pe.wait_ge(ctx_free[r], i * 6 + max(n - 2, 0))

                    def pT(block):
                        return probsT[:, 0, tile(block)], probsT[:, 1, tile(block)]

                    def v(buf, j):
                        return buf[:, 0, j, :], buf[:, 1, j, :]
                    if l < 2:
                        terms = [pT(2 * j + r) + v(val[s], j) for j in range(ROWS)]
                    else:
                        lower, upper, other = (3 * r + b for b in range(3))
                        terms = [pT(lower) + v(val_r, r), pT(upper) + v(val[s], r),
                                 pT(other) + v(val[s] if r == 0 else val_r, 1 - r)]
                    product(ctx_ps[:, r, 0:VW], terms).then_inc(ctx_filled, 1)

            def pair(i, items):
                for item in items:
                    stage, l, s, g = item
                    now = i - 1 if item in CARRIED else i
                    if (stage, l) in WEIGHTS_BY and s == 0 and g == 0:
                        pe.wait_ge(w_ready, WEIGHTS_BY[(stage, l)])
                    if stage == PROJECT:
                        project(now, item)
                    elif stage == VALUE:
                        values(now, item, 3 * l + 2, l)
                    elif stage == LEFT:
                        values(now, item, 3 * l, 3 * l - 4)
                    elif stage == SELF:
                        values(now, item, 3 * l + 1, 3 * l - 3)
                    elif stage == RIGHT:
                        values(now, item, 3 * l + 2, 3 * l - 2)
                    elif stage == OTHER:
                        score_other_side(now, item)
                    elif stage == SCORE:
                        (score_attention if l < 2 else score_convolution)(now, item)
                    elif stage == TURN_PROBS:
                        turn_probs(now, item)
                    elif stage == CONTEXT:
                        context(now, item)
                    elif stage == TURN:
                        turn(now, item)

            pe.wait_ge(pool_const, 1)
            pe.wait_ge(bias_ready, 1)
            run(pe, pair)

        @block.scalar
        def _(act):
            for w in range(NW):
                stage = arena[:, 2 * (w % 2):2 * (w % 2) + 2, :].rearrange("p a n -> p (a n)")[:, 0:KC * D]
                act.wait_ge(w_loaded[w % 2], 16 * (w // 2 + 1))
                nc.scalar.copy(w_hi[:, w, :, :].rearrange("p k d -> p (k d)"), stage).then_inc(w_hi_done, 1)

            def product_of(i, item):
                k = GEMM_AT[item]
                act.wait_ge(gemm_filled, i * GEMM_N + k + 1)
                return gemm_ps[k % GEMM_BANKS]

            def split_hi(i, item, dst, width=BANK):
                nc.scalar.copy(dst, product_of(i, item)[:, 0:width]).then_inc(hi_done, 1)

            def turn(i, item):
                _, l, s, _ = item
                hi = hT[s][:, 0, :, :].rearrange("p k r -> p (k r)")
                act.wait_ge(turn_filled, i * TURN_N + TURN_AT[item] + 1)
                if plain(l):
                    nc.scalar.copy(hi, turn_ps[:, 0:KC * S]).then_inc(turn_hi, 1)
                else:
                    for c in range(KC):
                        nc.scalar.activation(work[s][:, c * S:(c + 1) * S], turn_ps[:, c * S:(c + 1) * S],
                                             ACT.Relu, scale=ln_cols[:, l // 2, 0, c:c + 1],
                                             bias=ln_cols[:, l // 2, 1, c:c + 1]).then_inc(relu_done, 1)
                    act.wait_ge(relu_done, KC * (i * 4 + 2 * (l // 2) + s + 1))
                    nc.scalar.copy(hi, work[s]).then_inc(turn_hi, 1)

            def pair(i, items):
                for item in items:
                    stage, l, s, g = item
                    now = i - 1 if item in CARRIED else i
                    n = nth(item)
                    if stage == PROJECT:
                        split_hi(now, item, proj[:, 0, g * BANK:(g + 1) * BANK])
                    elif stage in (VALUE, LEFT):
                        split_hi(now, item, val[s][:, 0, g, 0:D], D)
                    elif stage == RIGHT:
                        split_hi(now, item, val_r[:, 0, g, 0:D], D)
                    elif stage == SELF:
                        bank = product_of(now, item)
                        nc.scalar.copy(z[s][:, g, :], bank[:, 0:D]).then_inc(gemm_free[GEMM_AT[item] % GEMM_BANKS], 1)
                    elif stage == SCORE and l < 2:
                        released(act, now, item)
                        flat = scores[:, :, :].rearrange("p r j -> p (r j)")
                        nc.scalar.activation(flat, flat, ACT.Exp, scale=SCALE).then_inc(exp_done, 1)
                    elif stage == SCORE:
                        k = GEMM_AT[item]
                        act.wait_ge(max_ready, now * 4 + n - 4 + 1)
                        bank = gemm_ps[k % GEMM_BANKS]
                        for r in range(ROWS):
                            last_exp = nc.scalar.activation(scores[:, r, :], bank[:, r * S:(r + 1) * S],
                                                            ACT.Exp, scale=SCALE, bias=col(s, NMAX + r, 1),
                                                            accum_out=col(s, Z + r, 1))
                        last_exp.then_inc(gemm_free[k % GEMM_BANKS], 1)
                    elif stage == TURN_PROBS:
                        act.wait_ge(turn_filled, now * TURN_N + TURN_AT[item] + 1)
                        nc.scalar.copy(probsT[:, 0, :], turn_ps[:, 0:6 * P]).then_inc(turn_hi, 1)
                    elif stage == NORM and l == 0:
                        act.wait_ge(rs_ready, now * 2 + s + 1)
                        nc.scalar.activation(z[s][:, 0, :], ctx_ps[:, 0, 0:D], ACT.Identity,
                                             scale=col(s, RS, 1), bias=col(s, NB, 1)).then_inc(z_ready[0], 1)
                    elif stage == TURN:
                        turn(now, item)

            act.wait_ge(const_loaded, 64)
            run(act, pair)

        @block.vector
        def _(dve):
            base = [0, 0]

            def step(ins):
                ins.then_inc(dve_step, 1)
                base[1] += 1
                return ins

            def settle():
                dve.wait_ge(dve_step, base[0] + base[1])

            vec = nc.vector
            step(vec.memset(exps[:, 0, :], 0.5))
            step(vec.memset(exps[:, 1, :], -0.5))
            for s in per:
                vec.memset(val[s][:, 0, :, D:VW].bitcast(F32), 1.0)
                vec.memset(val[s][:, 1, :, D:VW].bitcast(F32), 0.0)
            dve.wait_ge(const_loaded, 64)
            step(vec.tensor_scalar(bias_neg[:, :], bias_f[:, :], -1.0, None, ALU.mult))
            dve.wait_ge(pool_const, 1)
            settle()
            vec.tensor_copy(pick[:, :, :], pick_f[:, :].unsqueeze(2).to_broadcast([2 * NBIAS, NBIAS, P]))
            vec.scalar_tensor_tensor(bias_pair[:, :], bias_neg[:, :], half_sel[:, :], bias_f[:, :],
                                     ALU.mult, ALU.add).then_inc(bias_ready, 1)
            for w in range(NW):
                stage = arena[:, 2 * (w % 2):2 * (w % 2) + 2, :].rearrange("p a n -> p (a n)")[:, 0:KC * D]
                dve.wait_ge(w_hi_done, w + 1)
                vec.tensor_tensor(w_lo[:, w, :, :].rearrange("p k d -> p (k d)"), stage,
                                  w_hi[:, w, :, :].rearrange("p k d -> p (k d)"), ALU.subtract).then_inc(w_ready, 1)

            def split_lo(i, item, hi, lo, width=BANK):
                k = GEMM_AT[item]
                dve.wait_ge(hi_done, i * HI_N + HI_AT[item] + 1)
                vec.tensor_tensor(lo, gemm_ps[k % GEMM_BANKS][:, 0:width], hi, ALU.subtract)\
                   .then_inc(gemm_free[k % GEMM_BANKS], 1)

            def turn(i, item):
                _, l, s, _ = item
                dve.wait_ge(turn_hi, i * TURN_N + TURN_AT[item] + 1)
                hi = hT[s][:, 0, :, :].rearrange("p k r -> p (k r)")
                lo = hT[s][:, 1, :, :].rearrange("p k r -> p (k r)")
                whole = turn_ps[:, 0:KC * S] if plain(l) else work[s]
                vec.tensor_tensor(lo, whole, hi, ALU.subtract).then_inc(turn_free, 1)

            def blocks_flat(t):
                return t.rearrange("p r j -> p (r j)")

            def score_attention(i, item):
                _, l, s, _ = item
                n = nth(item)
                k = GEMM_AT[item]
                before = (OTHER, l, s, 0)
                other, own = gemm_ps[GEMM_AT[before] % GEMM_BANKS], gemm_ps[k % GEMM_BANKS]
                if l == 0:
                    dve.wait_ge(adj_loaded[s], 48 * (i + 1))
                    apart(dve)
                    step(vec.copy_predicated(blocks_flat(sym[s]), blocks_flat(from_adj), blocks_flat(adj[s])))
                dve.wait_ge(gemm_filled, i * GEMM_N + k + 1)
                apart(dve)
                diag = own[:, :].rearrange("p (a j) -> p a j", j=P)[:, 0:4:3, :]
                vec.copy_predicated(diag, take_side[:, :, :], other[:, 0:ROWS * P].rearrange("p (a j) -> p a j", j=P))\
                   .then_inc(gemm_free[GEMM_AT[before] % GEMM_BANKS], 1)
                released(dve, i, before)
                settle()
                vec.tensor_tensor(blocks_flat(scores), own[:, :], blocks_flat(sym[s]), ALU.mult)\
                   .then_inc(gemm_free[k % GEMM_BANKS], 1)
                dve.wait_ge(exp_done, i * 4 + n + 1)
                step(vec.tensor_tensor(blocks_flat(scores), blocks_flat(scores), blocks_flat(adjT[s]), ALU.mult))
                settle()
                hi, lo = probsT[:, 0, 0:4 * P], probsT[:, 1, 0:4 * P]
                vec.tensor_copy(hi, blocks_flat(scores)).then_inc(adjT_used[s], 1)
                dve.wait_ge(adjT_used[s], i * 2 + l + 1)
                vec.tensor_tensor(lo, blocks_flat(scores), hi, ALU.subtract).then_inc(probsT_ready, 1)

            def row_max(i, item):
                _, l, s, _ = item
                k = GEMM_AT[item]
                if l == 2:
                    for r in range(ROWS):
                        step(vec.scalar_tensor_tensor(junk[:, r, :], adj[s][:, r, r * P:(r + 1) * P], 1.0, ident[:, :],
                                                      ALU.mult, ALU.mult, accum_out=col(s, ADIAG + r, 1)))
                dve.wait_ge(gemm_filled, i * GEMM_N + k + 1)
                step(vec.tensor_reduce(col(s, MAXV), gemm_ps[k % GEMM_BANKS][:, :].rearrange("p (r j) -> p r j", r=ROWS),
                                       AX.X, ALU.max))
                settle()
                vec.tensor_scalar(col(s, NMAX), col(s, MAXV), -SCALE, None, ALU.mult).then_inc(max_ready, 1)

            def mask_probs(i, item):
                _, l, s, _ = item
                released(dve, i, (SCORE, l, s, 0))
                dve.wait_ge(tri_ready[s], i + 1)
                p = work[s].rearrange("p (r b j) -> p r b j", r=ROWS, b=3)
                e = scores[:, :, :]
                for r in range(ROWS):
                    e_diag = e[:, r, r * P:(r + 1) * P]
                    step(vec.scalar_tensor_tensor(junk[:, r, :], e_diag, 1.0, ident[:, :], ALU.mult, ALU.mult,
                                                  accum_out=col(s, PDIAG + r, 1)))
                    tri = adjT[s][:, r, :].rearrange("p (b j) -> p b j", b=2)
                    vec.tensor_tensor(p[:, r, 0:2, :], e_diag.unsqueeze(1).to_broadcast([P, 2, P]), tri, ALU.mult)
                flat_e, flat_a = blocks_flat(scores), blocks_flat(adj[s])
                vec.tensor_tensor(p[:, :, 2, :], flat_e[:, P:3 * P].rearrange("p (r j) -> p r j", r=ROWS),
                                  flat_a[:, P:3 * P].rearrange("p (r j) -> p r j", r=ROWS), ALU.mult)\
                   .then_inc(probs_ready, 1)
                settle()
                vec.tensor_tensor(col(s, PDIAG), col(s, PDIAG), col(s, ADIAG), ALU.mult).then_inc(adj_used[s], 1)
                dve.wait_ge(adj_used[s], i * 2 + l - 1)
                step(vec.scalar_tensor_tensor(col(s, QSUM), col(s, Z), 1e-10, col(s, PDIAG), ALU.mult, ALU.add))

            def mean_var(s, src, ready=dve_step):
                for r in range(ROWS):
                    step(vec.bn_stats(stats(s, r), src(r)))
                settle()
                apart(dve)
                for r in range(ROWS):
                    ins = vec.bn_aggr(small[s][:, MV + 2 * r:MV + 2 * r + 2], stats(s, r))
                    if ready is dve_step or r == 0:
                        step(ins)
                    else:
                        ins.then_inc(ready, 1)

            def outer_stats(s):
                mean_var(s, lambda r: z[s][:, r, :])
                settle()
                vec.tensor_scalar(col(s, VARP), variances(s), 1e-5, None, ALU.add).then_inc(var_ready, 1)

            def finish(i, item):
                _, l, s, _ = item
                dst = x_mid[s] if l == 1 else z[s]
                dve.wait_ge(pow_done, i * POW_N + POW_AT[item] + 1)
                for r in range(ROWS):
                    last = vec.tensor_scalar(dst[:, r, :], z[s][:, r, :], mean(s, r), col(s, ROOT + r, 1),
                                             ALU.subtract, ALU.mult)
                    if l == 1:
                        last.then_inc(z_ready[r], 1)
                if l == 3:
                    last.then_inc(y_ready[s], 1)

            def context_read(i, item):
                for r in range(ROWS):
                    dve.wait_ge(ctx_free[r], i * 6 + nth(item) - 1)

            def relu_residual(i, item, resid, src):
                _, l, s, _ = item
                for r in range(ROWS):
                    ins = vec.scalar_tensor_tensor(z[s][:, r, :], src(r), mean(s, r), ln_rows[:, l // 2, 0, :],
                                                   ALU.subtract, ALU.mult)
                    if l == 1:
                        ins.then_inc(ctx_free[r], 1)
                    else:
                        step(ins)
                if l == 1:
                    context_read(i, item)
                settle()
                for r in range(ROWS):
                    step(vec.scalar_tensor_tensor(z[s][:, r, :], z[s][:, r, :], col(s, RS + r, 1), ln_rows[:, l // 2, 1, :],
                                                  ALU.mult, ALU.add))
                settle()
                for r in range(ROWS):
                    ins = vec.scalar_tensor_tensor(z[s][:, r, :], z[s][:, r, :], 0.0, resid[:, r, :],
                                                   ALU.max, ALU.add)
                    if l == 1 and r == ROWS - 1:
                        ins.then_inc(resid_used[s], 1)
                    else:
                        step(ins)
                if l == 1:
                    dve.wait_ge(resid_used[s], i + 1)
                settle()

            def context_attention(i, item):
                _, l, s, _ = item
                dve.wait_ge(ctx_filled, i * 16 + 2 * nth(item) + 2)
                mean_var(s, lambda r: ctx_ps[:, r, 0:D], var_ready)
                step(vec.tensor_scalar(col(s, EPS), row_sums, 1e-3, 1e-13, ALU.mult, ALU.add))

            def norm_attention(i, item):
                _, l, s, _ = item
                dve.wait_ge(pow_done, i * POW_N + POW_AT[(CONTEXT, l, s, 0)] + 1)
                settle()
                step(vec.scalar_tensor_tensor(col(s, DEN), col(s, ROOT), (D / (D - 1.0)) ** 0.5, col(s, EPS),
                                              ALU.mult, ALU.add))
                settle()
                step(vec.reciprocal(col(s, RS), col(s, DEN)))
                settle()
                if l == 0:
                    vec.scalar_tensor_tensor(col(s, NB), means(s), -1.0, col(s, RS), ALU.mult, ALU.mult)\
                       .then_inc(rs_ready, 1)
                    vec.tensor_scalar(z[s][:, 1, :], ctx_ps[:, 1, 0:D], mean(s, 1), col(s, RS + 1, 1),
                                      ALU.subtract, ALU.mult).then_inc(z_ready[1], 1)
                else:
                    relu_residual(i, item, x_in[s], lambda r: ctx_ps[:, r, 0:D])
                    outer_stats(s)

            def context_convolution(i, item):
                _, l, s, _ = item
                dve.wait_ge(ctx_filled, i * 16 + 2 * nth(item) + 2)
                step(vec.tensor_tensor(col(s, QSUM), row_sums, col(s, QSUM), ALU.add))
                for r in range(ROWS):
                    released(dve, i, (SELF, l, s, r))
                    vec.scalar_tensor_tensor(z[s][:, r, :], z[s][:, r, :], col(s, PDIAG + r, 1),
                                             ctx_ps[:, r, 0:D], ALU.mult, ALU.add).then_inc(ctx_free[r], 1)
                context_read(i, item)
                settle()
                step(vec.scalar_tensor_tensor(col(s, EPS), col(s, QSUM), 1e-12, col(s, QSUM), ALU.mult, ALU.mult))
                mean_var(s, lambda r: z[s][:, r, :])
                settle()
                vec.tensor_tensor(col(s, VARP), variances(s), col(s, EPS), ALU.add).then_inc(var_ready, 1)

            def norm_convolution(i, item):
                _, l, s, _ = item
                dve.wait_ge(pow_done, i * POW_N + POW_AT[(CONTEXT, l, s, 0)] + 1)
                if l == 2:
                    for r in range(ROWS):
                        vec.tensor_scalar(z[s][:, r, :], z[s][:, r, :], mean(s, r), col(s, RS + r, 1),
                                          ALU.subtract, ALU.mult).then_inc(z_ready[r], 1)
                else:
                    relu_residual(i, item, x_mid[s], lambda r: z[s][:, r, :])
                    outer_stats(s)

            def pair(i, items):
                base[0] = start + i * DVE_STEPS - (CARRIED_STEPS if CARRIED[0] in items else 0)
                base[1] = 0
                for item in items:
                    stage, l, s, g = item
                    now = i - 1 if item in CARRIED else i
                    if stage == PROJECT:
                        at = slice(g * BANK, (g + 1) * BANK)
                        split_lo(now, item, proj[:, 0, at], proj[:, 1, at])
                    elif stage in (VALUE, LEFT):
                        split_lo(now, item, val[s][:, 0, g, 0:D], val[s][:, 1, g, 0:D], D)
                    elif stage == RIGHT:
                        if l == 2 and s == 0 and g == 0:
                            vec.memset(val_r[:, 0, :, D:VW].bitcast(F32), 1.0)
                            vec.memset(val_r[:, 1, :, D:VW].bitcast(F32), 0.0)
                        split_lo(now, item, val_r[:, 0, g, 0:D], val_r[:, 1, g, 0:D], D)
                    elif stage == SCORE:
                        (score_attention if l < 2 else row_max)(now, item)
                    elif stage == MASK:
                        mask_probs(now, item)
                    elif stage == TURN_PROBS:
                        dve.wait_ge(turn_hi, now * TURN_N + TURN_AT[item] + 1)
                        vec.tensor_tensor(probsT[:, 1, :], turn_ps[:, 0:6 * P], probsT[:, 0, :], ALU.subtract)\
                           .then_inc(turn_free, 1)
                    elif stage == CONTEXT:
                        (context_attention if l < 2 else context_convolution)(now, item)
                    elif stage == NORM:
                        (norm_attention if l < 2 else norm_convolution)(now, item)
                    elif stage == FINISH:
                        finish(now, item)
                    elif stage == TURN:
                        turn(now, item)
                assert base[1] == sum(STEPS.get(item[:2], 0) for item in items)

            start = base[1]
            run(dve, pair)

        @block.gpsimd
        def _(pool):
            gp = nc.gpsimd
            gp.memset(ident[:, :], 0.0).then_inc(pool_step, 1)
            gp.memset(half_sel[:, :], 1.0).then_inc(pool_step, 1)
            gp.memset(pick_f[:, :], 0.0).then_inc(pool_step, 1)
            gp.memset(from_adj[:, :, :], 1.0).then_inc(pool_step, 1)
            gp.memset(take_side[:, :, :], 1.0).then_inc(pool_step, 1)
            pool.wait_ge(pool_step, 5)
            gp.affine_select(out=ident[:, :], in_=ident[:, :], compare_op=ALU.not_equal, fill=1.0, base=0,
                             pattern=[[-1, P]], channel_multiplier=1)
            gp.affine_select(out=half_sel[:, :], in_=half_sel[:, :], compare_op=ALU.is_ge, fill=0.0, base=-NBIAS,
                             pattern=[[0, 1]], channel_multiplier=1)
            gp.affine_select(out=pick_f[:, :], in_=pick_f[:, :], compare_op=ALU.not_equal, fill=1.0, base=0,
                             pattern=[[-1, NBIAS]], channel_multiplier=1).then_inc(pool_step, 1)
            pool.wait_ge(pool_step, 6)
            gp.affine_select(out=pick_f[:, :], in_=pick_f[:, :], compare_op=ALU.not_equal, fill=1.0, base=-NBIAS,
                             pattern=[[-1, NBIAS]], channel_multiplier=1)
            gp.affine_select(out=from_adj[:, :, :], in_=from_adj[:, :, :], compare_op=ALU.is_gt, fill=0.0, base=0,
                             pattern=[[-P, ROWS], [1, S]], channel_multiplier=-1)
            gp.affine_select(out=take_side[:, 0, :], in_=take_side[:, 0, :], compare_op=ALU.is_ge, fill=0.0, base=0,
                             pattern=[[-1, P]], channel_multiplier=1)
            gp.affine_select(out=take_side[:, 1, :], in_=take_side[:, 1, :], compare_op=ALU.is_gt, fill=0.0, base=0,
                             pattern=[[1, P]], channel_multiplier=-1).then_inc(pool_const, 1)

            def power(i, item):
                stage, l, s, _ = item
                src, dst, exponent = col(s, VARP), col(s, ROOT), exps[:, 1, :]
                if stage == CONTEXT and l < 2:
                    src, exponent = variances(s), exps[:, 0, :]
                elif stage == CONTEXT:
                    dst = col(s, RS)
                pool.wait_ge(var_ready, i * POW_N + POW_AT[item] + 1)
                gp.tensor_tensor(dst, src, exponent, ALU.pow).then_inc(pow_done, 1)

            def pair(i, items):
                for item in items:
                    stage, l, s, _ = item
                    now = i - 1 if item in CARRIED else i
                    if stage == CONTEXT and l == 0 and CARRIED[0] in items:
                        pool.wait_ge(y_stored[s], 16 * i)
                    if stage in (CONTEXT, FINISH):
                        power(now, item)
                    if stage == FINISH and l == 3:
                        pool.wait_ge(y_ready[s], now + 1)
                        gp.dma_start(out_d[now, s].rearrange("r p d -> p r d"), z[s][:, :, :]).then_inc(y_stored[s], 16)
                    if stage == SCORE and l == 1:
                        pool.wait_ge(adjT_used[s], 2 * now + 2)
                        apart(pool)
                        for r in range(ROWS):
                            a = adj[s][:, r, r * P:(r + 1) * P]
                            gp.affine_select(out=adjT[s][:, r, 0:P], in_=a, compare_op=ALU.is_gt, fill=0.0, base=0,
                                             pattern=[[-1, P]], channel_multiplier=1)
                            tri = gp.affine_select(out=adjT[s][:, r, P:S], in_=a, compare_op=ALU.is_gt, fill=0.0,
                                                   base=0, pattern=[[1, P]], channel_multiplier=-1)
                        tri.then_inc(tri_ready[s], 1)

            run(pool, pair)
            for s in per:
                pool.wait_ge(y_stored[s], 16 * PAIRS)


WEIGHTS_BY = {(PROJECT, 0): 2, (VALUE, 0): 3, (PROJECT, 1): 5, (VALUE, 1): 6,
              (LEFT, 2): 7, (SELF, 2): 8, (RIGHT, 2): 9, (LEFT, 3): 10, (SELF, 3): 11, (RIGHT, 3): 12}


def kernel(x, adj, L0_gnn_W_left, L0_gnn_W_right, L0_gnn_W_lin, L0_gnn_b_lin, L0_gnn_ln_a, L0_gnn_ln_b,
           L1_gnn_Wl, L1_gnn_bl, L1_gnn_Ws, L1_gnn_bs, L1_gnn_Wr, L1_gnn_br, L1_gnn_ln_w, L1_gnn_ln_b):
    import numpy as np
    import concourse.bacc as bacc
    from concourse.bass_utils import run_bass_kernel_spmd

    f = lambda a: np.ascontiguousarray(np.asarray(a))
    t = lambda a: np.swapaxes(np.asarray(a), -1, -2)
    grid = (PAIRS, STREAMS, ROWS, P)
    weights = []
    for l in range(2):
        weights += [t(L0_gnn_W_left[l]), t(L0_gnn_W_right[l]), t(L0_gnn_W_lin[l])]
    for l in range(2):
        weights += [t(L1_gnn_Wl[l]), t(L1_gnn_Ws[l]), t(L1_gnn_Wr[l])]
    biases = [L0_gnn_b_lin[0], L0_gnn_b_lin[1]]
    for l in range(2):
        biases += [L1_gnn_bl[l], L1_gnn_bs[l], L1_gnn_br[l]]
    cols = [[L0_gnn_ln_a[0], L0_gnn_ln_b[0]], [L1_gnn_ln_w[0], L1_gnn_ln_b[0]]]
    rows = [[L0_gnn_ln_a[1], L0_gnn_ln_b[1]], [L1_gnn_ln_w[1], L1_gnn_ln_b[1]]]
    arrays = {
        "x_dram": f(x).reshape(grid + (D,)),
        "adj_dram": f(adj).reshape(grid + (S,)),
        "adjT_dram": f(t(adj)).reshape(grid + (S,)),
        "w_dram": f(np.stack([np.asarray(w) for w in weights])),
        "bias_dram": f(np.stack([np.asarray(b) for b in biases])),
        "lncol_dram": f(np.asarray(np.stack([[np.asarray(c) for c in p] for p in cols])).reshape(2, 2, KC, P).transpose(3, 0, 1, 2)),
        "lnrow_dram": f(np.stack([[np.asarray(c) for c in p] for p in rows])),
    }
    nc = bacc.Bacc("TRN2", target_bir_lowering=False, num_devices=1)
    args = [nc.dram_tensor(n, a.shape, mybir.dt.from_np(a.dtype), kind="ExternalInput").ap() for n, a in arrays.items()]
    out = nc.dram_tensor("out_dram", grid + (D,), F32, kind="ExternalOutput").ap()
    build(nc, *args, out)
    r = run_bass_kernel_spmd(nc, [arrays], core_ids=[0])
    return r.results[0]["out_dram"].reshape(B, S, D)
```

```python
import concourse.bass as bass
from concourse import mybir
from contextlib import ExitStack

F32 = mybir.dt.float32
F32R = mybir.dt.float32r
I8 = mybir.dt.int8
ALU = mybir.AluOpType
ACT = mybir.ActivationFunctionType
AX = mybir.AxisListType

P = 128
B, S, D = 32, 256, 384
ROWS = S // P
KC = D // P
STREAMS = 2
PAIRS = B // STREAMS
LAYERS = 4
VW = D + 2
SCALE = 1.0 / float(D) ** 0.5
GEMM_BANKS = 4
BANK = 512

PROJECT, VALUE, OTHER, SCORE = "project", "value", "score_other_side", "score"
LEFT, SELF, RIGHT = "value_left", "value_self", "value_right"
GEMMS = (PROJECT, VALUE, OTHER, SCORE, LEFT, SELF, RIGHT)
TURN, TURN_PROBS, CONTEXT = "turn", "turn_probs", "context"
ATTEND, MASK, MERGE, NORM, RESID, STATS, FINISH = "attend", "mask", "merge", "norm", "resid", "stats", "finish"
WEIGHT = "weight"
BIAS = "bias"


PROGRAMS = {
    "pe": """
        turn/in/0 context/3/1 project/0/0/0 project/0/0/1 project/0/0/2 value/0/0/0 score_other_side/0/0
        turn/in/1 score/0/0 value/0/0/1 project/0/1/0 project/0/1/1 context/0/0 project/0/1/2 value/0/1/0
        score_other_side/0/1 turn/0/0 score/0/1 value/0/1/1 project/1/0/0 project/1/0/1 context/0/1
        project/1/0/2 value/1/0/0 score_other_side/1/0 turn/0/1 score/1/0 value/1/0/1 project/1/1/0
        project/1/1/1 context/1/0 project/1/1/2 value/1/1/0 score_other_side/1/1 score/1/1 turn/1/0 value/1/1/1
        score/2/0 context/1/1 value_right/2/0/0 value_left/2/0/0 value_left/2/0/1 turn_probs/2/0
        value_right/2/0/1 value_self/2/0/0 context/2/0 turn/1/1 value_self/2/0/1 score/2/1 value_left/2/1/0
        value_left/2/1/1 value_right/2/1/0 value_self/2/1/1 turn/2/0 value_right/2/1/1 value_self/2/1/0
        turn_probs/2/1 score/3/0 context/2/1 value_left/3/0/0 value_left/3/0/1 value_right/3/0/0 turn/2/1
        value_right/3/0/1 value_self/3/0/0 value_self/3/0/1 turn_probs/3/0 score/3/1 context/3/0
        value_left/3/1/0 value_left/3/1/1 value_right/3/1/1 value_right/3/1/0 value_self/3/1/1 turn_probs/3/1
        value_self/3/1/0
    """,
    "act": """
        turn/in/0 finish/3/0 project/0/0/0 project/0/0/1 project/0/0/2 value/0/0/0 score_other_side/0/0
        turn/in/1 attend/0/0 value/0/0/1 project/0/1/0 project/0/1/1 project/0/1/2 finish/3/1 value/0/1/0
        norm/0/0 score_other_side/0/1 turn/0/0 attend/0/1 value/0/1/1 project/1/0/0 project/1/0/1 project/1/0/2
        norm/0/1 value/1/0/0 score_other_side/1/0 turn/0/1 attend/1/0 value/1/0/1 project/1/1/0 project/1/1/1
        project/1/1/2 value/1/1/0 score_other_side/1/1 finish/1/0 turn/1/0 attend/1/1 value/1/1/1 score/2/0
        value_right/2/0/0 value_left/2/0/0 value_left/2/0/1 turn_probs/2/0 value_right/2/0/1 value_self/2/0/0
        finish/1/1 turn/1/1 value_self/2/0/1 score/2/1 norm/2/0 value_left/2/1/0 value_left/2/1/1
        value_right/2/1/0 turn/2/0 value_right/2/1/1 value_self/2/1/0 turn_probs/2/1 value_self/2/1/1 score/3/0
        value_left/3/0/0 norm/2/1 value_left/3/0/1 value_right/3/0/0 turn/2/1 value_right/3/0/1 value_self/3/0/0
        value_self/3/0/1 turn_probs/3/0 score/3/1 value_left/3/1/0 value_left/3/1/1 value_right/3/1/1
        value_right/3/1/0 value_self/3/1/1 turn_probs/3/1 value_self/3/1/0
    """,
    "dve": """
        turn/in/0 finish/3/0 merge/3/1 project/0/0/0 project/0/0/1 project/0/0/2 value/0/0/0
        score_other_side/0/0 norm/3/1 turn/in/1 score/0/0 resid/3/1 attend/0/0 value/0/0/1 stats/3/1
        project/0/1/0 project/0/1/1 context/0/0 project/0/1/2 finish/3/1 norm/0/0 value/0/1/0
        score_other_side/0/1 turn/0/0 score/0/1 attend/0/1 value/0/1/1 project/1/0/0 project/1/0/1 context/0/1
        project/1/0/2 norm/0/1 value/1/0/0 score_other_side/1/0 turn/0/1 score/1/0 attend/1/0 value/1/0/1
        project/1/1/0 project/1/1/1 context/1/0 norm/1/0 resid/1/0 project/1/1/2 stats/1/0 value/1/1/0
        score_other_side/1/1 finish/1/0 score/1/1 turn/1/0 value/1/1/1 attend/1/1 score/2/0 context/1/1 norm/1/1
        mask/2/0 resid/1/1 value_right/2/0/0 value_left/2/0/0 value_left/2/0/1 turn_probs/2/0 value_right/2/0/1
        stats/1/1 value_self/2/0/0 finish/1/1 turn/1/1 value_self/2/0/1 merge/2/0 score/2/1 value_left/2/1/0
        value_left/2/1/1 mask/2/1 value_right/2/1/0 turn/2/0 value_right/2/1/1 value_self/2/1/0 turn_probs/2/1
        value_self/2/1/1 score/3/0 merge/2/1 value_left/3/0/0 value_left/3/0/1 mask/3/0 value_right/3/0/0
        turn/2/1 value_right/3/0/1 value_self/3/0/0 value_self/3/0/1 turn_probs/3/0 score/3/1 merge/3/0
        value_left/3/1/0 norm/3/0 value_left/3/1/1 mask/3/1 resid/3/0 value_right/3/1/0 value_self/3/1/1
        value_right/3/1/1 turn_probs/3/1 value_self/3/1/0 stats/3/0
    """,
}


def stage_of(word):
    stage, layer, stream, part = (word.split("/") + ["0"])[:4]
    return stage, -1 if layer == "in" else int(layer), int(stream), int(part)


TAKES = {engine: [stage_of(word) for word in text.split()] for engine, text in PROGRAMS.items()}
CARRIED = [(FINISH, LAYERS - 1, 0, 0)] + [(k, LAYERS - 1, 1, 0) for k in (CONTEXT, MERGE, NORM, RESID, STATS, FINISH)]
NW = 12
CHUNKS = NW * KC
AHEAD = 2 * KC


def first_order(order):
    chunks = list(range(AHEAD, CHUNKS))
    out = []
    for item in order:
        if item in CARRIED:
            continue
        out.append(item)
        if item == (PROJECT, 0, 0, 0):
            out.append((BIAS, 0, 0, 0))
        if item[0] in (TURN, PROJECT, VALUE):
            n = 1 if item[0] != TURN and item[3] else 2
            out += [(WEIGHT, c, 0, 0) for c in chunks[:n]]
            del chunks[:n]
    return out


def ordinals(engine, kinds, which=lambda item: True):
    items = [item for item in [o for o in TAKES[engine] if o not in CARRIED] + CARRIED if item[0] in kinds and which(item)]
    return {item: n for n, item in enumerate(items)}, len(items)


GEMM_AT, GEMM_N = ordinals("pe", GEMMS)
HI_AT, HI_N = ordinals("act", (PROJECT, VALUE, LEFT, RIGHT))
TURN_AT, TURN_N = ordinals("pe", (TURN, TURN_PROBS))
POW_AT, POW_N = ordinals("dve", (CONTEXT, MERGE, STATS), lambda item: item[0] != CONTEXT or item[1] < 2)
SELF_AT, SELF_N = ordinals("dve", (SELF,))
SHIFT_AT, SHIFT_N = ordinals("dve", (MERGE, STATS), lambda item: item[0] == STATS or item[1] == 2)
TURN_HI_AT, TURN_HI_N = ordinals("act", (TURN, TURN_PROBS), lambda item: item[0] == TURN_PROBS or item[1] in (-1, 1))
STEPS = {(PROJECT, 0): 3, (SCORE, 0): 1, (SCORE, 1): 1, (ATTEND, 0): 1, (ATTEND, 1): 1,
         (SCORE, 2): 1, (SCORE, 3): 1, (MASK, 2): 3, (MASK, 3): 3,
         (CONTEXT, 0): 5, (CONTEXT, 1): 4, (MERGE, 2): 7, (MERGE, 3): 8,
         (NORM, 0): 2, (NORM, 1): 4, (NORM, 3): 2, (RESID, 1): 1, (RESID, 3): 2, (STATS, 1): 5, (STATS, 3): 5}


def steps(items):
    return sum(STEPS.get(item[:2], 0) for item in items if item[0] != PROJECT or item[3] == 0)


DVE_STEPS, CARRIED_STEPS = steps(TAKES["dve"]), steps(CARRIED)
assert GEMM_N % GEMM_BANKS == 0
BANK_N = GEMM_N // GEMM_BANKS


def build(nc, x_d, adj_d, adjT_d, w_d, bias_d, lncol_d, lnrow_d, out_d):
    ctx = ExitStack()
    with ctx:
        def sb(name, shape, dt=F32):
            return ctx.enter_context(nc.sbuf_tensor(name, shape, dt))

        def ps(name, shape):
            return ctx.enter_context(nc.psum_tensor(name, shape, F32))

        def sem(name):
            return ctx.enter_context(nc.semaphore(name))

        w_hi = sb("w_hi", [P, NW, KC, D], F32R)
        w_lo = sb("w_lo", [P, NW, KC, D], F32R)
        NBIAS = 8
        bias_pair = sb("bias_pair", [2 * NBIAS, D], F32R)
        self_rows = sb("self_rows", [P, 2, D])
        pick = sb("pick", [2 * NBIAS, NBIAS, P], F32R)
        pick_f = sb("pick_f", [2 * NBIAS, NBIAS])
        half_sel = sb("half_sel", [2 * NBIAS, 1])
        ln_rows = sb("ln_rows", [P, 2, 2, D])
        ln_cols = sb("ln_cols", [P, 2, 2, KC])
        ident = sb("ident", [P, P])
        from_adj = sb("from_adj", [P, ROWS, S], I8)
        take_side = sb("take_side", [P, ROWS, P], I8)
        exps = sb("exps", [P, 2, 2])

        proj = sb("proj", [P, 2, 6 * S + 8], F32R)
        scores = sb("scores", [P, ROWS, S])
        probsT = sb("probsT", [P, 2, 6 * P], F32R)

        bias_f = scores[:, :, :].rearrange("p r j -> p (r j)")[0:2 * NBIAS, 0:D]
        bias_neg = probsT[0:2 * NBIAS, 0, 0:D]

        per = range(STREAMS)
        arena = sb("arena", [P, 2 * STREAMS, ROWS * D])
        z = [arena[:, s, :].rearrange("p (r d) -> p r d", r=ROWS) for s in per]
        work = [arena[:, STREAMS + s, :] for s in per]
        hT = [sb(f"hT{s}", [P, 2, KC, S], F32R) for s in per]
        val = [sb(f"val{s}", [P, 2, ROWS, VW], F32R) for s in per]
        adj = [sb(f"adj{s}", [P, ROWS, S]) for s in per]
        adjT = [sb(f"adjT{s}", [P, ROWS, S]) for s in per]
        sym = [sb(f"sym{s}", [P, ROWS, S]) for s in per]
        x_in = [sb(f"x_in{s}", [P, ROWS, D]) for s in per]
        x_mid = [sb(f"x_mid{s}", [P, ROWS, D]) for s in per]
        small = [sb(f"small{s}", [P, 64]) for s in per]
        other_side = sb("other_side", [P, ROWS, P])
        junk = sb("junk", [P, ROWS, P])

        val_r = proj[:, :, 0:ROWS * VW].rearrange("p h (r v) -> p h r v", r=ROWS)

        def col(s, first, n=ROWS):
            return small[s][:, first:first + n]
        BN, MV, ROOT, RS, NB, EPS, DEN = 0, 12, 16, 18, 20, 22, 24
        ADIAG, PDIAG, Z, NMAX, MAXV, QSUM, VARP, NMEAN = 26, 28, 30, 32, 34, 36, 38, 40

        def stats(s, r):
            return small[s][:, BN + 6 * r:BN + 6 * r + 6]

        def mean(s, r):
            return small[s][:, MV + 2 * r:MV + 2 * r + 1]

        def means(s):
            return small[s][:, MV:MV + 4].rearrange("p (r c) -> p r c", c=2)[:, :, 0]

        def variances(s):
            return small[s][:, MV:MV + 4].rearrange("p (r c) -> p r c", c=2)[:, :, 1]

        gemm_ps = [ps(f"gemm_ps{b}", [P, BANK]) for b in range(GEMM_BANKS)]
        turn_ps = ps("turn_ps", [P, 2 * BANK])
        ctx_ps = ps("ctx_ps", [P, ROWS, BANK])
        row_sums = ctx_ps[:, :, D]

        x_loaded = [sem(f"x_loaded{s}") for s in per]
        adj_loaded = [sem(f"adj_loaded{s}") for s in per]
        resid_used = [sem(f"resid_used{s}") for s in per]
        adj_used = [sem(f"adj_used{s}") for s in per]
        attn_hi_done = [sem(f"attn_hi_done{s}") for s in per]
        tri_ready = [sem(f"tri_ready{s}") for s in per]
        slots = [arena[:, n // 2, (n % 2) * D:(n % 2 + 1) * D] for n in range(8)] \
            + [x_mid[n // 2][:, n % 2, :] for n in range(4)]
        ring = len(slots) - 8

        def slot(n):
            return (n, 0) if n < 8 else (8 + (n - 8) % ring, (n - 8) // ring)

        w_loaded = [sem(f"w_loaded{i}") for i in range(len(slots))]
        w_hi_done = sem("w_hi_done")
        w_ready = sem("w_ready")
        bias_loaded = sem("bias_loaded")
        const_loaded = sem("const_loaded")
        pool_const = sem("pool_const")
        pool_step = sem("pool_step")
        waited = sem("waited")
        bias_ready = sem("bias_ready")
        gemm_filled = sem("gemm_filled")
        gemm_free = [sem(f"gemm_free{b}") for b in range(GEMM_BANKS)]
        self_ready = sem("self_ready")
        hi_done = sem("hi_done")
        max_ready = sem("max_ready")
        other_copied = sem("other_copied")
        exp_done = sem("exp_done")
        probs_ready = sem("probs_ready")
        probsT_ready = sem("probsT_ready")
        turn_filled = sem("turn_filled")
        turn_hi = sem("turn_hi")
        relu_done = sem("relu_done")
        chunk_hi_done = sem("chunk_hi_done")
        turn_free = sem("turn_free")
        ctx_filled = sem("ctx_filled")
        ctx_free = [sem(f"ctx_free{r}") for r in range(ROWS)]
        var_ready = sem("var_ready")
        pow_done = sem("pow_done")
        shift_done = sem("shift_done")
        rs_ready = sem("rs_ready")
        z_ready = [sem(f"z_ready{r}") for r in range(ROWS)]
        y_ready = [sem(f"y_ready{s}") for s in per]
        y_stored = [sem(f"y_stored{s}") for s in per]
        dve_step = sem("dve_step")

        block = ctx.enter_context(nc.Block())

        def halves(bank):
            return bank[:, :].rearrange("p (r h j) -> p r h j", r=ROWS, h=2)

        def nth(item):
            return 2 * item[1] + item[2]

        def released(engine, i, item):
            k = GEMM_AT[item]
            engine.wait_ge(gemm_free[k % GEMM_BANKS], i * BANK_N + k // GEMM_BANKS + 1)

        def apart(engine):
            engine.sem_inc(waited, 1)

        def plain(layer):
            return layer in (-1, 1)

        def run(engine, pair, order):
            pair(0, first_order(order))
            with engine.Fori(1, PAIRS) as i:
                pair(i, order)
            pair(PAIRS, [item for item in order if item in CARRIED])

        @block.sync
        def _(sp):
            def load_x(s, i):
                sp.dma_start(x_in[s][:, :, :], x_d[i, s].rearrange("r p d -> p r d")).then_inc(x_loaded[s], 16)

            def load_adj(s, i):
                a, t = (m[i, s].rearrange("r p j -> p r j") for m in (adj_d, adjT_d))
                sp.dma_start(adj[s][:, :, :], a).then_inc(adj_loaded[s], 16)
                sp.dma_start(adjT[s][:, :, :], t).then_inc(adj_loaded[s], 16)
                sp.dma_start(sym[s][:, :, :], t).then_inc(adj_loaded[s], 16)

            def load_chunk(n):
                at, use = slot(n)
                if use:
                    sp.wait_ge(w_ready, n - ring + 1)
                sp.dma_start(slots[at], w_d[n // KC, (n % KC) * P:(n % KC + 1) * P, :]).then_inc(w_loaded[at], 16)

            load_x(0, 0)
            for n in range(AHEAD):
                load_chunk(n)
            sp.dma_start(bias_f[0:NBIAS], bias_d).then_inc(bias_loaded, 16)
            sp.dma_start(bias_f[NBIAS:2 * NBIAS], bias_d).then_inc(bias_loaded, 16)
            for n in range(AHEAD, 8):
                load_chunk(n)
            load_x(1, 0)
            load_adj(0, 0)
            sp.dma_start(ln_cols[:, :, :, :], lncol_d).then_inc(const_loaded, 16)
            sp.dma_start(ln_rows[:, :, :, :], lnrow_d.partition_broadcast(P)).then_inc(const_loaded, 16)
            sp.dma_start(self_rows[:, :, :], bias_d[3:7:3, :].partition_broadcast(P)).then_inc(const_loaded, 16)
            for n in range(8, 12):
                load_chunk(n)
            load_adj(1, 0)
            for n in range(12, CHUNKS):
                load_chunk(n)
            with sp.Fori(1, PAIRS) as i:
                for s in per:
                    sp.wait_ge(resid_used[s], i)
                    load_x(s, i)
                for s in per:
                    sp.wait_ge(adj_used[s], 2 * i)
                    load_adj(s, i)

        @block.tensor
        def _(pe):
            def product(out, terms, late=(), before_late=None, before_term=None):
                first, last = [], []
                for n, t in enumerate(terms):
                    if len(t) == 4:
                        s_hi, s_lo, m_hi, m_lo = t
                        for p, (st, mv) in enumerate(((s_hi, m_hi), (s_hi, m_lo), (s_lo, m_hi))):
                            (last if p in late else first).append((n, st, mv))
                    else:
                        first.append((n,) + t)
                waited_for = -1
                for done, (n, st, mv) in enumerate(first + last):
                    if before_term is not None and n > waited_for:
                        before_term(n)
                        waited_for = n
                    if before_late is not None and done == len(first):
                        before_late()
                    ins = nc.tensor.matmul(out, st, mv, start=(done == 0), stop=(done == len(first + last) - 1))
                return ins

            def weight(w, k, cols):
                return w_hi[:, w, k, cols], w_lo[:, w, k, cols]

            def features(s, k, rows):
                return hT[s][:, 0, k, rows], hT[s][:, 1, k, rows]

            def tile(r):
                return slice(r * P, (r + 1) * P)

            def bank(i, item):
                k = GEMM_AT[item]
                pe.wait_ge(gemm_free[k % GEMM_BANKS], i * BANK_N + k // GEMM_BANKS)
                return gemm_ps[k % GEMM_BANKS]

            def featured(i, item):
                _, l, s, _ = item
                pe.wait_ge(turn_free, i * TURN_N + TURN_AT[(TURN, l - 1, s, 0)] + 1)

            def featured_hi(i, item, k):
                _, l, s, _ = item
                if not plain(l - 1):
                    pe.wait_ge(chunk_hi_done, KC * (i * 4 + 2 * ((l - 1) // 2) + s) + k + 1)
                elif k == 0:
                    pe.wait_ge(turn_hi, i * TURN_HI_N + TURN_HI_AT[(TURN, l - 1, s, 0)] + 1)

            def project(i, item):
                _, l, s, g = item
                featured(i, item)
                out = bank(i, item)
                for half in range(2):
                    side, o = divmod(2 * g + half, KC)
                    last = product(out[:, half * S:(half + 1) * S],
                                   [weight(3 * l + side, k, tile(o)) + features(s, k, slice(0, S)) for k in range(KC)])
                last.then_inc(gemm_filled, 1)

            def values(i, item, w, bias=None):
                _, l, s, r = item
                featured(i, item)
                out = bank(i, item)
                product(out[:, 0:D],
                        [features(s, k, tile(r)) + weight(w, k, slice(0, D)) for k in range(KC)]
                        + ([] if bias is None else [(pick[:, bias, :], bias_pair[:, :])])).then_inc(gemm_filled, 1)

            def projected(side, k, r):
                at = slice((side * KC + k) * S + r * P, (side * KC + k) * S + (r + 1) * P)
                return proj[:, 0, at], proj[:, 1, at]

            def score_other_side(i, item):
                _, l, s, _ = item
                out = bank(i, item)
                for r in range(ROWS):
                    both, high = out[:, 2 * r * P:(2 * r + 2) * P], out[:, 2 * r * P:(2 * r + 1) * P]
                    pe.wait_ge(hi_done, i * HI_N + HI_AT[(PROJECT, l, s, 1 + r)] + 1)
                    for k in range(KC):
                        nc.tensor.matmul(both, projected(r, k, r)[0], hT[s][:, :, k, tile(r)], start=(k == 0), stop=False)
                    for g in range(2) if r == 0 else (2,):
                        released(pe, i, (PROJECT, l, s, g))
                    for k in range(KC):
                        last = nc.tensor.matmul(high, projected(r, k, r)[1], hT[s][:, 0, k, tile(r)],
                                                start=False, stop=(k == KC - 1))
                last.then_inc(gemm_filled, 1)

            def score_attention(i, item):
                _, l, s, _ = item
                out = bank(i, item)
                for r in range(ROWS):
                    last = product(out[:, r * S:(r + 1) * S],
                                   [projected(1 - r, k, r) + features(s, k, slice(0, S)) for k in range(KC)])
                last.then_inc(gemm_filled, 1)

            def score_convolution(i, item):
                _, l, s, _ = item
                out = bank(i, item)
                for r in range(ROWS):
                    ahead = ((1, 2), lambda: featured(i, item), lambda k: featured_hi(i, item, k)) if r == 0 else ()
                    last = product(out[:, r * S:(r + 1) * S],
                                   [features(s, k, tile(r)) + features(s, k, slice(0, S)) for k in range(KC)], *ahead)
                last.then_inc(gemm_filled, 1)

            def turn_probs(i, item):
                _, l, s, _ = item
                pe.wait_ge(probs_ready, i * 4 + 2 * (l - 2) + s + 1)
                pe.wait_ge(turn_free, i * TURN_N + TURN_AT[item])
                for b in range(6):
                    last = nc.tensor.transpose(turn_out(b), work[s][:, tile(b)], ident[:, :])
                last.then_inc(turn_filled, 1)

            def turn_out(b):
                return turn_ps[:, b * P:(b + 1) * P]

            def turn(i, item):
                _, l, s, _ = item
                src = {-1: x_in, 0: z, 1: x_mid, 2: z}[l][s]
                pe.wait_ge(turn_free, i * TURN_N + TURN_AT[item])
                if l == -1:
                    pe.wait_ge(x_loaded[s], 16 * (i + 1))
                for r in range(ROWS):
                    if l >= 0:
                        pe.wait_ge(z_ready[r], i * 6 + 2 * l + s + 1)
                    for c in range(KC):
                        last = nc.tensor.transpose(turn_ps[:, c * S + r * P:c * S + (r + 1) * P],
                                                   src[:, r, tile(c)], ident[:, :])
                last.then_inc(turn_filled, 1)

            def context(i, item):
                _, l, s, _ = item
                n = nth(item)
                if l < 2:
                    pe.wait_ge(attn_hi_done[s], i * 2 + l + 1)
                    released(pe, i, (VALUE, l, s, 1))
                else:
                    pe.wait_ge(turn_hi, i * TURN_HI_N + TURN_HI_AT[(TURN_PROBS, l, s, 0)] + 1)
                    released(pe, i, (LEFT, l, s, 1))
                    released(pe, i, (RIGHT, l, s, 1))

                def split():
                    if l < 2:
                        pe.wait_ge(probsT_ready, i * 4 + n + 1)
                    else:
                        pe.wait_ge(turn_free, i * TURN_N + TURN_AT[(TURN_PROBS, l, s, 0)] + 1)
                for r in range(ROWS):
                    if n in (1, 2):
                        pe.wait_ge(z_ready[r], i * 6 + n)
                    else:
                        pe.wait_ge(ctx_free[r], i * 6 + max(n - 2, 0))

                    def pT(block):
                        return probsT[:, 0, tile(block)], probsT[:, 1, tile(block)]

                    def v(buf, j):
                        return buf[:, 0, j, :], buf[:, 1, j, :]
                    if l < 2:
                        terms = [pT(2 * j + r) + v(val[s], j) for j in range(ROWS)]
                    else:
                        lower, upper, other = (3 * r + b for b in range(3))
                        terms = [pT(lower) + v(val_r, r), pT(upper) + v(val[s], r),
                                 pT(other) + v(val[s] if r == 0 else val_r, 1 - r)]
                    product(ctx_ps[:, r, 0:VW], terms, *(((2,), split) if r == 0 else ())).then_inc(ctx_filled, 1)

            def pair(i, items):
                for item in items:
                    stage, l, s, g = item
                    now = i - 1 if item in CARRIED else i
                    if (stage, l) in WEIGHTS_BY and s == 0 and g == 0:
                        pe.wait_ge(w_ready, KC * WEIGHTS_BY[(stage, l)])
                        if stage == VALUE:
                            pe.wait_ge(bias_ready, 2)
                    if stage == PROJECT:
                        project(now, item)
                    elif stage == VALUE:
                        values(now, item, 3 * l + 2, l)
                    elif stage == LEFT:
                        values(now, item, 3 * l, 3 * l - 4)
                    elif stage == SELF:
                        values(now, item, 3 * l + 1)
                    elif stage == RIGHT:
                        values(now, item, 3 * l + 2, 3 * l - 2)
                    elif stage == OTHER:
                        score_other_side(now, item)
                    elif stage == SCORE:
                        (score_attention if l < 2 else score_convolution)(now, item)
                    elif stage == TURN_PROBS:
                        turn_probs(now, item)
                    elif stage == CONTEXT:
                        context(now, item)
                    elif stage == TURN:
                        turn(now, item)

            pe.wait_ge(pool_const, 1)
            run(pe, pair, TAKES["pe"])

        @block.scalar
        def _(act):
            def chunk_hi(n):
                at, use = slot(n)
                act.wait_ge(w_loaded[at], 16 * (use + 1))
                nc.scalar.copy(w_hi[:, n // KC, n % KC, :], slots[at]).then_inc(w_hi_done, 1)

            def product_of(i, item):
                k = GEMM_AT[item]
                act.wait_ge(gemm_filled, i * GEMM_N + k + 1)
                return gemm_ps[k % GEMM_BANKS]

            def split_hi(i, item, dst, width=BANK):
                nc.scalar.copy(dst, product_of(i, item)[:, 0:width]).then_inc(hi_done, 1)

            def normalise(s, r, dst, src, scale):
                return nc.scalar.activation(dst[:, r, :], src, ACT.Identity, scale=col(s, scale + r, 1),
                                            bias=col(s, NB + r, 1))

            def turn(i, item):
                _, l, s, _ = item
                hi = hT[s][:, 0, :, :].rearrange("p k r -> p (k r)")
                act.wait_ge(turn_filled, i * TURN_N + TURN_AT[item] + 1)
                if plain(l):
                    nc.scalar.copy(hi, turn_ps[:, 0:KC * S]).then_inc(turn_hi, 1)
                else:
                    act.wait_ge(const_loaded, 48)
                    before = KC * (i * 4 + 2 * (l // 2) + s)
                    for c in range(KC + 1):
                        if c < KC:
                            nc.scalar.activation(work[s][:, c * S:(c + 1) * S], turn_ps[:, c * S:(c + 1) * S],
                                                 ACT.Relu, scale=ln_cols[:, l // 2, 0, c:c + 1],
                                                 bias=ln_cols[:, l // 2, 1, c:c + 1]).then_inc(relu_done, 1)
                        if c:
                            act.wait_ge(relu_done, before + c)
                            nc.scalar.copy(hi[:, (c - 1) * S:c * S], work[s][:, (c - 1) * S:c * S])\
                              .then_inc(chunk_hi_done, 1)

            def pair(i, items):
                for item in items:
                    stage, l, s, g = item
                    now = i - 1 if item in CARRIED else i
                    n = nth(item)
                    if stage == PROJECT:
                        split_hi(now, item, proj[:, 0, g * BANK:(g + 1) * BANK])
                    elif stage in (VALUE, LEFT):
                        split_hi(now, item, val[s][:, 0, g, 0:D], D)
                    elif stage == RIGHT:
                        split_hi(now, item, val_r[:, 0, g, 0:D], D)
                    elif stage == SELF:
                        bank = product_of(now, item)
                        nc.scalar.copy(z[s][:, g, :], bank[:, 0:D]).then_inc(gemm_free[GEMM_AT[item] % GEMM_BANKS], 1)
                    elif stage == OTHER:
                        nc.scalar.copy(other_side[:, :, :], halves(product_of(now, item))[:, :, 0, :])\
                          .then_inc(other_copied, 1)
                    elif stage == ATTEND:
                        released(act, now, (SCORE, l, s, 0))
                        flat = scores[:, :, :].rearrange("p r j -> p (r j)")
                        nc.scalar.activation(flat, flat, ACT.Exp, scale=SCALE).then_inc(exp_done, 1)
                    elif stage == SCORE and l >= 2:
                        k = GEMM_AT[item]
                        act.wait_ge(max_ready, now * 4 + n - 4 + 1)
                        bank = gemm_ps[k % GEMM_BANKS]
                        for r in range(ROWS):
                            last_exp = nc.scalar.activation(scores[:, r, :], bank[:, r * S:(r + 1) * S],
                                                            ACT.Exp, scale=SCALE, bias=col(s, NMAX + r, 1),
                                                            accum_out=col(s, Z + r, 1))
                        last_exp.then_inc(gemm_free[k % GEMM_BANKS], 1)
                    elif stage == TURN_PROBS:
                        act.wait_ge(turn_filled, now * TURN_N + TURN_AT[item] + 1)
                        nc.scalar.copy(probsT[:, 0, :], turn_ps[:, 0:6 * P]).then_inc(turn_hi, 1)
                    elif stage == NORM and l == 0:
                        act.wait_ge(rs_ready, now * 2 + s + 1)
                        for r in range(ROWS):
                            normalise(s, r, z[s], ctx_ps[:, r, 0:D], RS).then_inc(z_ready[r], 1)
                    elif stage == NORM and l == 2:
                        act.wait_ge(shift_done, now * SHIFT_N + SHIFT_AT[(MERGE, l, s, 0)] + 1)
                        for r in range(ROWS):
                            normalise(s, r, z[s], z[s][:, r, :], RS).then_inc(z_ready[r], 1)
                    elif stage == FINISH and l == 1:
                        act.wait_ge(shift_done, now * SHIFT_N + SHIFT_AT[(STATS, l, s, 0)] + 1)
                        normalise(s, 1, x_mid[s], z[s][:, 1, :], ROOT).then_inc(z_ready[1], 1)
                    elif stage == FINISH:
                        act.wait_ge(shift_done, now * SHIFT_N + SHIFT_AT[(STATS, l, s, 0)] + 1)
                        for r in range(ROWS):
                            last = normalise(s, r, z[s], z[s][:, r, :], ROOT)
                        last.then_inc(y_ready[s], 1)
                    elif stage == TURN:
                        turn(now, item)
                    elif stage == WEIGHT:
                        chunk_hi(l)

            for n in range(AHEAD):
                chunk_hi(n)
            run(act, pair, TAKES["act"])

        @block.vector
        def _(dve):
            base = [0, 0]

            def step(ins):
                ins.then_inc(dve_step, 1)
                base[1] += 1
                return ins

            def settle():
                dve.wait_ge(dve_step, base[0] + base[1])

            vec = nc.vector
            step(vec.memset(exps[:, 0, :], 0.5))
            step(vec.memset(exps[:, 1, :], -0.5))
            for s in per:
                vec.memset(val[s][:, 0, :, D:VW].bitcast(F32), 1.0)
                vec.memset(val[s][:, 1, :, D:VW].bitcast(F32), 0.0)
            dve.wait_ge(pool_const, 1)

            def split_biases():
                dve.wait_ge(bias_loaded, 32)
                vec.tensor_scalar(bias_neg, bias_f, -1.0, None, ALU.mult).then_inc(bias_ready, 1)
                vec.tensor_copy(pick[:, :, :], pick_f[:, :].unsqueeze(2).to_broadcast([2 * NBIAS, NBIAS, P]))
                dve.wait_ge(bias_ready, 1)
                vec.scalar_tensor_tensor(bias_pair[:, :], bias_neg, half_sel[:, :], bias_f,
                                         ALU.mult, ALU.add).then_inc(bias_ready, 1)

            def chunk_lo(n):
                dve.wait_ge(w_hi_done, n + 1)
                vec.tensor_tensor(w_lo[:, n // KC, n % KC, :], slots[slot(n)[0]], w_hi[:, n // KC, n % KC, :],
                                  ALU.subtract).then_inc(w_ready, 1)

            for n in range(AHEAD):
                chunk_lo(n)

            def split_lo(i, item, hi, lo, width=BANK):
                k = GEMM_AT[item]
                dve.wait_ge(hi_done, i * HI_N + HI_AT[item] + 1)
                vec.tensor_tensor(lo, gemm_ps[k % GEMM_BANKS][:, 0:width], hi, ALU.subtract)\
                   .then_inc(gemm_free[k % GEMM_BANKS], 1)

            def turn(i, item):
                _, l, s, _ = item
                hi = hT[s][:, 0, :, :].rearrange("p k r -> p (k r)")
                lo = hT[s][:, 1, :, :].rearrange("p k r -> p (k r)")
                if plain(l):
                    dve.wait_ge(turn_hi, i * TURN_HI_N + TURN_HI_AT[item] + 1)
                    vec.tensor_tensor(lo, turn_ps[:, 0:KC * S], hi, ALU.subtract).then_inc(turn_free, 1)
                else:
                    for c in range(KC):
                        at = slice(c * S, (c + 1) * S)
                        dve.wait_ge(chunk_hi_done, KC * (i * 4 + 2 * (l // 2) + s) + c + 1)
                        last = vec.tensor_tensor(lo[:, at], work[s][:, at], hi[:, at], ALU.subtract)
                    last.then_inc(turn_free, 1)

            def blocks_flat(t):
                return t.rearrange("p r j -> p (r j)")

            def symmetric_mask(i, s):
                dve.wait_ge(adj_loaded[s], 48 * (i + 1))
                apart(dve)
                step(vec.copy_predicated(blocks_flat(sym[s]), blocks_flat(from_adj), blocks_flat(adj[s])))
                for r in range(ROWS):
                    step(vec.scalar_tensor_tensor(junk[:, r, :], adj[s][:, r, r * P:(r + 1) * P], 1.0, ident[:, :],
                                                  ALU.mult, ALU.mult, accum_out=col(s, ADIAG + r, 1)))

            def add_other_side(i, item):
                k = GEMM_AT[item]
                dve.wait_ge(other_copied, i * 4 + nth(item) + 1)
                vec.tensor_tensor(other_side[:, :, :], halves(gemm_ps[k % GEMM_BANKS])[:, :, 1, :],
                                  other_side[:, :, :], ALU.add)\
                   .then_inc(gemm_free[k % GEMM_BANKS], 1)

            def score_attention(i, item):
                _, l, s, _ = item
                k = GEMM_AT[item]
                before = (OTHER, l, s, 0)
                own = gemm_ps[k % GEMM_BANKS]
                dve.wait_ge(gemm_filled, i * GEMM_N + k + 1)
                released(dve, i, before)
                apart(dve)
                diag = own[:, :].rearrange("p (a j) -> p a j", j=P)[:, 0:4:3, :]
                step(vec.copy_predicated(diag, take_side[:, :, :], other_side[:, :, :]))
                settle()
                vec.tensor_tensor(blocks_flat(scores), own[:, :], blocks_flat(sym[s]), ALU.mult)\
                   .then_inc(gemm_free[k % GEMM_BANKS], 1)

            def attend(i, item):
                _, l, s, _ = item
                dve.wait_ge(exp_done, i * 4 + nth(item) + 1)
                step(vec.tensor_tensor(blocks_flat(scores), blocks_flat(scores), blocks_flat(adjT[s]), ALU.mult))
                settle()
                hi, lo = probsT[:, 0, 0:4 * P], probsT[:, 1, 0:4 * P]
                vec.tensor_copy(hi, blocks_flat(scores)).then_inc(attn_hi_done[s], 1)
                dve.wait_ge(attn_hi_done[s], i * 2 + l + 1)
                vec.tensor_tensor(lo, blocks_flat(scores), hi, ALU.subtract).then_inc(probsT_ready, 1)

            def row_max(i, item):
                _, l, s, _ = item
                k = GEMM_AT[item]
                dve.wait_ge(gemm_filled, i * GEMM_N + k + 1)
                step(vec.tensor_reduce(col(s, MAXV), gemm_ps[k % GEMM_BANKS][:, :].rearrange("p (r j) -> p r j", r=ROWS),
                                       AX.X, ALU.max))
                settle()
                vec.tensor_scalar(col(s, NMAX), col(s, MAXV), -SCALE, None, ALU.mult).then_inc(max_ready, 1)

            def mask_probs(i, item):
                _, l, s, _ = item
                released(dve, i, (SCORE, l, s, 0))
                dve.wait_ge(tri_ready[s], i + 1)
                p = work[s].rearrange("p (r b j) -> p r b j", r=ROWS, b=3)
                e = scores[:, :, :]
                for r in range(ROWS):
                    e_diag = e[:, r, r * P:(r + 1) * P]
                    step(vec.scalar_tensor_tensor(junk[:, r, :], e_diag, 1.0, ident[:, :], ALU.mult, ALU.mult,
                                                  accum_out=col(s, PDIAG + r, 1)))
                    tri = adjT[s][:, r, :].rearrange("p (b j) -> p b j", b=2)
                    vec.tensor_tensor(p[:, r, 0:2, :], e_diag.unsqueeze(1).to_broadcast([P, 2, P]), tri, ALU.mult)
                flat_e, flat_a = blocks_flat(scores), blocks_flat(adj[s])
                vec.tensor_tensor(p[:, :, 2, :], flat_e[:, P:3 * P].rearrange("p (r j) -> p r j", r=ROWS),
                                  flat_a[:, P:3 * P].rearrange("p (r j) -> p r j", r=ROWS), ALU.mult)\
                   .then_inc(probs_ready, 1)
                settle()
                vec.tensor_tensor(col(s, PDIAG), col(s, PDIAG), col(s, ADIAG), ALU.mult).then_inc(adj_used[s], 1)
                dve.wait_ge(adj_used[s], i * 2 + l - 1)
                step(vec.scalar_tensor_tensor(col(s, QSUM), col(s, Z), 1e-10, col(s, PDIAG), ALU.mult, ALU.add))

            def mean_var(s, src, ready=dve_step, filled=None):
                for r in range(ROWS):
                    if filled is not None:
                        dve.wait_ge(ctx_filled, filled + r)
                    step(vec.bn_stats(stats(s, r), src(r)))
                settle()
                apart(dve)
                for r in range(ROWS):
                    ins = vec.bn_aggr(small[s][:, MV + 2 * r:MV + 2 * r + 2], stats(s, r))
                    if ready is dve_step or r == 0:
                        step(ins)
                    else:
                        ins.then_inc(ready, 1)

            def outer_stats(i, item):
                _, l, s, _ = item
                if l == 1:
                    dve.wait_ge(resid_used[s], i + 1)
                settle()
                mean_var(s, lambda r: z[s][:, r, :])
                settle()
                step(vec.tensor_scalar(col(s, NMEAN), means(s), -1.0, None, ALU.mult))
                vec.tensor_scalar(col(s, VARP), variances(s), 1e-5, None, ALU.add).then_inc(var_ready, 1)

            def finish(i, item):
                _, l, s, _ = item
                dve.wait_ge(pow_done, i * POW_N + POW_AT[(STATS, l, s, 0)] + 1)
                vec.tensor_scalar(x_mid[s][:, 0, :], z[s][:, 0, :], mean(s, 0), col(s, ROOT, 1),
                                  ALU.subtract, ALU.mult).then_inc(z_ready[0], 1)

            def context_read(i, item):
                for r in range(ROWS):
                    dve.wait_ge(ctx_free[r], i * 6 + nth(item) - 1)

            def centre(i, item, src):
                _, l, s, _ = item
                for r in range(ROWS):
                    ins = vec.scalar_tensor_tensor(z[s][:, r, :], src(r), mean(s, r), ln_rows[:, l // 2, 0, :],
                                                   ALU.subtract, ALU.mult)
                    if l == 1:
                        ins.then_inc(ctx_free[r], 1)
                    else:
                        step(ins)

            def scale_shift(i, item):
                _, l, s, _ = item
                if l == 1:
                    context_read(i, item)
                settle()
                for r in range(ROWS):
                    step(vec.scalar_tensor_tensor(z[s][:, r, :], z[s][:, r, :], col(s, RS + r, 1), ln_rows[:, l // 2, 1, :],
                                                  ALU.mult, ALU.add))

            def relu_residual(i, item):
                _, l, s, _ = item
                resid = x_in[s] if l == 1 else x_mid[s]
                for r in range(ROWS):
                    dve.wait_ge(dve_step, base[0] + base[1] - (ROWS - 1))
                    ins = vec.scalar_tensor_tensor(z[s][:, r, :], z[s][:, r, :], 0.0, resid[:, r, :],
                                                   ALU.max, ALU.add)
                    if l == 1 and r == ROWS - 1:
                        ins.then_inc(resid_used[s], 1)
                    else:
                        step(ins)

            def context_attention(i, item):
                _, l, s, _ = item
                if l == 1:
                    dve.wait_ge(const_loaded, 48)
                mean_var(s, lambda r: ctx_ps[:, r, 0:D], var_ready, i * 16 + 2 * nth(item) + 1)
                step(vec.tensor_scalar(col(s, EPS), row_sums, 1e-3, 1e-13, ALU.mult, ALU.add))
                dve.wait_ge(var_ready, i * POW_N + POW_AT[item] + 1)
                settle()
                if l == 0:
                    step(vec.tensor_scalar(col(s, NMEAN), means(s), -1.0, None, ALU.mult))
                else:
                    centre(i, item, lambda r: ctx_ps[:, r, 0:D])

            def norm_attention(i, item):
                _, l, s, _ = item
                dve.wait_ge(pow_done, i * POW_N + POW_AT[(CONTEXT, l, s, 0)] + 1)
                settle()
                step(vec.scalar_tensor_tensor(col(s, DEN), col(s, ROOT), (D / (D - 1.0)) ** 0.5, col(s, EPS),
                                              ALU.mult, ALU.add))
                settle()
                step(vec.reciprocal(col(s, RS), col(s, DEN)))
                settle()
                if l == 0:
                    vec.tensor_tensor(col(s, NB), col(s, NMEAN), col(s, RS), ALU.mult)\
                       .then_inc(rs_ready, 1)
                else:
                    scale_shift(i, item)

            def merge(i, item):
                _, l, s, _ = item
                for r in range(ROWS):
                    dve.wait_ge(self_ready, i * SELF_N + SELF_AT[(SELF, l, s, r)] + 1)
                    dve.wait_ge(ctx_filled, i * 16 + 2 * nth(item) + 1 + r)
                    if r == ROWS - 1:
                        step(vec.tensor_tensor(col(s, QSUM), row_sums, col(s, QSUM), ALU.add))
                    vec.scalar_tensor_tensor(z[s][:, r, :], z[s][:, r, :], col(s, PDIAG + r, 1),
                                             ctx_ps[:, r, 0:D], ALU.mult, ALU.add).then_inc(ctx_free[r], 1)
                context_read(i, item)
                settle()
                step(vec.scalar_tensor_tensor(col(s, EPS), col(s, QSUM), 1e-12, col(s, QSUM), ALU.mult, ALU.mult))
                mean_var(s, lambda r: z[s][:, r, :])
                settle()
                if l == 2:
                    step(vec.tensor_scalar(col(s, NMEAN), means(s), -1.0, None, ALU.mult))
                vec.tensor_tensor(col(s, VARP), variances(s), col(s, EPS), ALU.add).then_inc(var_ready, 1)
                if l == 3:
                    centre(i, item, lambda r: z[s][:, r, :])

            def norm_convolution(i, item):
                _, l, s, _ = item
                if l == 3:
                    dve.wait_ge(pow_done, i * POW_N + POW_AT[(MERGE, l, s, 0)] + 1)
                    scale_shift(i, item)

            def pair(i, items):
                base[0] = start + i * DVE_STEPS - (CARRIED_STEPS if CARRIED[-1] in items else 0)
                base[1] = 0
                for item in items:
                    stage, l, s, g = item
                    now = i - 1 if item in CARRIED else i
                    if stage == PROJECT:
                        at = slice(g * BANK, (g + 1) * BANK)
                        split_lo(now, item, proj[:, 0, at], proj[:, 1, at])
                        if l == 0 and g == 0:
                            symmetric_mask(now, s)
                    elif stage in (VALUE, LEFT):
                        split_lo(now, item, val[s][:, 0, g, 0:D], val[s][:, 1, g, 0:D], D)
                    elif stage == RIGHT:
                        if l == 2 and s == 0 and g == 0:
                            vec.memset(val_r[:, 0, :, D:VW].bitcast(F32), 1.0)
                            vec.memset(val_r[:, 1, :, D:VW].bitcast(F32), 0.0)
                        split_lo(now, item, val_r[:, 0, g, 0:D], val_r[:, 1, g, 0:D], D)
                    elif stage == SCORE:
                        (score_attention if l < 2 else row_max)(now, item)
                    elif stage == MASK:
                        mask_probs(now, item)
                    elif stage == TURN_PROBS:
                        dve.wait_ge(turn_hi, now * TURN_HI_N + TURN_HI_AT[item] + 1)
                        vec.tensor_tensor(probsT[:, 1, :], turn_ps[:, 0:6 * P], probsT[:, 0, :], ALU.subtract)\
                           .then_inc(turn_free, 1)
                    elif stage == CONTEXT and l < 2:
                        context_attention(now, item)
                    elif stage == MERGE:
                        merge(now, item)
                    elif stage == NORM:
                        (norm_attention if l < 2 else norm_convolution)(now, item)
                    elif stage == OTHER:
                        add_other_side(now, item)
                    elif stage == ATTEND:
                        attend(now, item)
                    elif stage == RESID:
                        relu_residual(now, item)
                    elif stage == STATS:
                        outer_stats(now, item)
                    elif stage == FINISH and l == 1:
                        finish(now, item)
                    elif stage == TURN:
                        turn(now, item)
                    elif stage == BIAS:
                        split_biases()
                    elif stage == WEIGHT:
                        chunk_lo(l)
                assert base[1] == steps(items)

            start = base[1]
            run(dve, pair, TAKES["dve"])

        @block.gpsimd
        def _(pool):
            gp = nc.gpsimd
            gp.memset(ident[:, :], 0.0).then_inc(pool_step, 1)
            gp.memset(half_sel[:, :], 1.0).then_inc(pool_step, 1)
            gp.memset(pick_f[:, :], 0.0).then_inc(pool_step, 1)
            gp.memset(from_adj[:, :, :], 1.0).then_inc(pool_step, 1)
            gp.memset(take_side[:, :, :], 1.0).then_inc(pool_step, 1)
            pool.wait_ge(pool_step, 5)
            gp.affine_select(out=ident[:, :], in_=ident[:, :], compare_op=ALU.not_equal, fill=1.0, base=0,
                             pattern=[[-1, P]], channel_multiplier=1)
            gp.affine_select(out=half_sel[:, :], in_=half_sel[:, :], compare_op=ALU.is_ge, fill=0.0, base=-NBIAS,
                             pattern=[[0, 1]], channel_multiplier=1)
            gp.affine_select(out=pick_f[:, :], in_=pick_f[:, :], compare_op=ALU.not_equal, fill=1.0, base=0,
                             pattern=[[-1, NBIAS]], channel_multiplier=1).then_inc(pool_step, 1)
            pool.wait_ge(pool_step, 6)
            gp.affine_select(out=pick_f[:, :], in_=pick_f[:, :], compare_op=ALU.not_equal, fill=1.0, base=-NBIAS,
                             pattern=[[-1, NBIAS]], channel_multiplier=1)
            gp.affine_select(out=from_adj[:, :, :], in_=from_adj[:, :, :], compare_op=ALU.is_gt, fill=0.0, base=0,
                             pattern=[[-P, ROWS], [1, S]], channel_multiplier=-1)
            gp.affine_select(out=take_side[:, 0, :], in_=take_side[:, 0, :], compare_op=ALU.is_ge, fill=0.0, base=0,
                             pattern=[[-1, P]], channel_multiplier=1)
            gp.affine_select(out=take_side[:, 1, :], in_=take_side[:, 1, :], compare_op=ALU.is_gt, fill=0.0, base=0,
                             pattern=[[1, P]], channel_multiplier=-1).then_inc(pool_const, 1)

            def power(i, item):
                stage, l, s, _ = item
                src, dst, exponent = col(s, VARP), col(s, ROOT), exps[:, 1, :]
                if stage == CONTEXT and l < 2:
                    src, exponent = variances(s), exps[:, 0, :]
                elif stage == MERGE:
                    dst = col(s, RS)
                pool.wait_ge(var_ready, i * POW_N + POW_AT[item] + 1)
                gp.tensor_tensor(dst, src, exponent, ALU.pow).then_inc(pow_done, 1)
                if item in SHIFT_AT:
                    pool.wait_ge(pow_done, i * POW_N + POW_AT[item] + 1)
                    gp.tensor_tensor(col(s, NB), col(s, NMEAN), dst, ALU.mult).then_inc(shift_done, 1)

            def pair(i, items):
                for item in items:
                    stage, l, s, g = item
                    now = i - 1 if item in CARRIED else i
                    if stage == CONTEXT and l == 0 and CARRIED[-1] in items:
                        pool.wait_ge(y_stored[s], 16 * i)
                    if item in POW_AT:
                        power(now, item)
                    if stage == SELF:
                        released(pool, now, item)
                        gp.tensor_tensor(z[s][:, g, :], z[s][:, g, :], self_rows[:, l - 2, :],
                                         ALU.add).then_inc(self_ready, 1)
                    if stage == FINISH and l == 3:
                        pool.wait_ge(y_ready[s], now + 1)
                        gp.dma_start(out_d[now, s].rearrange("r p d -> p r d"), z[s][:, :, :]).then_inc(y_stored[s], 16)
                    if stage == ATTEND and l == 1:
                        pool.wait_ge(attn_hi_done[s], 2 * now + 2)
                        apart(pool)
                        for r in range(ROWS):
                            a = adj[s][:, r, r * P:(r + 1) * P]
                            gp.affine_select(out=adjT[s][:, r, 0:P], in_=a, compare_op=ALU.is_gt, fill=0.0, base=0,
                                             pattern=[[-1, P]], channel_multiplier=1)
                            tri = gp.affine_select(out=adjT[s][:, r, P:S], in_=a, compare_op=ALU.is_gt, fill=0.0,
                                                   base=0, pattern=[[1, P]], channel_multiplier=-1)
                        tri.then_inc(tri_ready[s], 1)

            pool.wait_ge(const_loaded, 48)
            run(pool, pair, TAKES["dve"])
            for s in per:
                pool.wait_ge(y_stored[s], 16 * PAIRS)


WEIGHTS_BY = {(PROJECT, 0): 2, (VALUE, 0): 3, (PROJECT, 1): 5, (VALUE, 1): 6,
              (LEFT, 2): 7, (SELF, 2): 8, (RIGHT, 2): 9, (LEFT, 3): 10, (SELF, 3): 11, (RIGHT, 3): 12}


def kernel(x, adj, L0_gnn_W_left, L0_gnn_W_right, L0_gnn_W_lin, L0_gnn_b_lin, L0_gnn_ln_a, L0_gnn_ln_b,
           L1_gnn_Wl, L1_gnn_bl, L1_gnn_Ws, L1_gnn_bs, L1_gnn_Wr, L1_gnn_br, L1_gnn_ln_w, L1_gnn_ln_b):
    import numpy as np
    import concourse.bacc as bacc
    from concourse.bass_utils import run_bass_kernel_spmd

    f = lambda a: np.ascontiguousarray(np.asarray(a))
    t = lambda a: np.swapaxes(np.asarray(a), -1, -2)
    grid = (PAIRS, STREAMS, ROWS, P)
    weights = []
    for l in range(2):
        weights += [t(L0_gnn_W_left[l]), t(L0_gnn_W_right[l]), t(L0_gnn_W_lin[l])]
    for l in range(2):
        weights += [t(L1_gnn_Wl[l]), t(L1_gnn_Ws[l]), t(L1_gnn_Wr[l])]
    biases = [L0_gnn_b_lin[0], L0_gnn_b_lin[1]]
    for l in range(2):
        biases += [L1_gnn_bl[l], L1_gnn_bs[l], L1_gnn_br[l]]
    cols = [[L0_gnn_ln_a[0], L0_gnn_ln_b[0]], [L1_gnn_ln_w[0], L1_gnn_ln_b[0]]]
    rows = [[L0_gnn_ln_a[1], L0_gnn_ln_b[1]], [L1_gnn_ln_w[1], L1_gnn_ln_b[1]]]
    arrays = {
        "x_dram": f(x).reshape(grid + (D,)),
        "adj_dram": f(adj).reshape(grid + (S,)),
        "adjT_dram": f(t(adj)).reshape(grid + (S,)),
        "w_dram": f(np.stack([np.asarray(w) for w in weights])),
        "bias_dram": f(np.stack([np.asarray(b) for b in biases])),
        "lncol_dram": f(np.stack([[np.asarray(c) for c in p] for p in cols]).reshape(2, 2, KC, P).transpose(3, 0, 1, 2)),
        "lnrow_dram": f(np.stack([[np.asarray(c) for c in p] for p in rows])),
    }
    nc = bacc.Bacc("TRN2", target_bir_lowering=False, num_devices=1)
    args = [nc.dram_tensor(n, a.shape, mybir.dt.from_np(a.dtype), kind="ExternalInput").ap() for n, a in arrays.items()]
    out = nc.dram_tensor("out_dram", grid + (D,), F32, kind="ExternalOutput").ap()
    build(nc, *args, out)
    r = run_bass_kernel_spmd(nc, [arrays], core_ids=[0])
    return r.results[0]["out_dram"].reshape(B, S, D)
```
